# Optimizing a Trainium2 kernel written in Bass

```python
import numpy as np
import jax
import jax.numpy as jnp

def _softmax(x, axis=-1):
    return jax.nn.softmax(x, axis=axis)

def _gelu(x):
    return jax.nn.gelu(x, approximate=True)

def _silu(x):
    return jax.nn.silu(x)

def _sigmoid(x):
    return jax.nn.sigmoid(x)

def _layernorm(x, axis=-1, eps=1e-05):
    m = jnp.mean(x, axis=axis, keepdims=True)
    v = jnp.var(x, axis=axis, keepdims=True)
    return (x - m) / jnp.sqrt(v + eps)

def _scatter_add(tgt, idx, src, axis=0):
    return tgt.at[idx].add(src)

def _segment_sum(src, seg, n):
    return jax.ops.segment_sum(src, seg, n)
kernel_name = 'mk_adj_resnorm_d2_adj_r2_f175dc'

def setup_inputs(seed: int=0):
    np.random.seed(seed)
    _w = jnp.asarray

    def _rec_inputs():
        import jax
        import jax.numpy as jnp
        _gk = jax.random.key(seed)
        x = 7.22e-05 + 1 * jax.random.normal(jax.random.fold_in(_gk, 1), (4096, 256), jnp.float32)
        _w = (1.0 + jnp.arange(4096, dtype=jnp.float32)) ** (-0.5)
        _w = _w / _w.mean()
        _pij = jnp.clip(0.00195312 * _w[:, None] * _w[None, :], 0.0, 1.0)
        _a = jax.random.uniform(jax.random.fold_in(_gk, 2), (4096, 4096)) < _pij
        _a = jnp.logical_or(_a, jnp.eye(4096, dtype=bool))
        _af = _a.astype(jnp.float32)
        _af = _af * jax.random.uniform(jax.random.fold_in(_gk, 3), (4096, 4096), jnp.float32, 0.05, 1)
        adj = _af
        return (x, adj)
    x, adj = _rec_inputs()

    def _L0_gnn_setup():
        import jax, jax.numpy as jnp
        import numpy as np
        N, NFEAT, NHID = (8192, 256, 256)

        def _gc_layer(x, adj, W):
            support = adj @ x
            h = jnp.concatenate([x, support], axis=1)
            return h @ W
        key = jax.random.key(seed)
        k1, k2, k3, k4 = jax.random.split(key, 4)
        x = jax.random.normal(k1, (N, NFEAT), dtype=jnp.float32)
        adj = jax.random.uniform(k2, (N, N), dtype=jnp.float32)
        stdv1 = 1.0 / np.sqrt(NHID)
        W1 = jax.random.uniform(k3, (2 * NFEAT, NHID), dtype=jnp.float32, minval=-stdv1, maxval=stdv1)
        W2 = jax.random.uniform(k4, (2 * NHID, NHID), dtype=jnp.float32, minval=-stdv1, maxval=stdv1)
        return {'x': x, 'adj': adj, 'W1': W1, 'W2': W2}
    _L0_gnn_all = _L0_gnn_setup()
    _L0_gnn_in = {k: v for k, v in _L0_gnn_all.items() if k in ('W1', 'W2')}
    del _L0_gnn_all

    def _L1_gnn_setup():
        import jax, jax.numpy as jnp
        import numpy as np
        N = 4096
        D_IN = 256
        D_OUT = 256
        EDGE_P = 0.004

        def _xavier_uniform(key, fan_in, fan_out):
            bound = np.sqrt(6.0 / (fan_in + fan_out))
            return jax.random.uniform(key, (fan_in, fan_out), jnp.float32, -bound, bound)
        key = jax.random.key(seed)
        kx, ks, kw, ku = jax.random.split(key, 4)
        x = jax.random.normal(kx, (N, D_IN), dtype=jnp.float32)
        S = (jax.random.uniform(ks, (N, N), dtype=jnp.float32) < EDGE_P).astype(jnp.float32)
        W = _xavier_uniform(kw, D_IN, D_OUT)
        U = _xavier_uniform(ku, D_OUT, D_OUT)
        return {'x': x, 'S': S, 'W': W, 'U': U}
    _L1_gnn_all = _L1_gnn_setup()
    _L1_gnn_in = {k: v for k, v in _L1_gnn_all.items() if k in ('W', 'U')}
    del _L1_gnn_all
    return {'x': x, 'adj': adj, 'L0_gnn_W1': _L0_gnn_in['W1'], 'L0_gnn_W2': _L0_gnn_in['W2'], 'L1_gnn_W': _L1_gnn_in['W'], 'L1_gnn_U': _L1_gnn_in['U']}

def reference(x, adj, L0_gnn_W1, L0_gnn_W2, L1_gnn_W, L1_gnn_U):
    import jax
    import jax.numpy as jnp

    def _L0_gnn_ref(x, adj, W1, W2):
        import jax, jax.numpy as jnp
        import numpy as np
        N, NFEAT, NHID = (8192, 256, 256)

        def _gc_layer(x, adj, W):
            support = adj @ x
            h = jnp.concatenate([x, support], axis=1)
            return h @ W
        h = jax.nn.relu(_gc_layer(x, adj, W1))
        h = jax.nn.relu(_gc_layer(h, adj, W2))
        return h

    def _L1_gnn_ref(x, S, W, U):
        import jax, jax.numpy as jnp
        import numpy as np
        N = 4096
        D_IN = 256
        D_OUT = 256
        EDGE_P = 0.004

        def _xavier_uniform(key, fan_in, fan_out):
            bound = np.sqrt(6.0 / (fan_in + fan_out))
            return jax.random.uniform(key, (fan_in, fan_out), jnp.float32, -bound, bound)
        n = x.shape[0]
        S = S + jnp.eye(n, dtype=S.dtype)
        h = x @ W
        scores = h @ U @ h.T
        mask = S > 0
        scores = jnp.where(mask, scores, -jnp.inf)
        att = jax.nn.softmax(scores, axis=-1)
        att = att * mask.astype(att.dtype)
        S_tilde = S * att
        return S_tilde @ h
    x = _layernorm(x + _L0_gnn_ref(x, adj, L0_gnn_W1, L0_gnn_W2), axis=-1)
    x = _layernorm(x + _L1_gnn_ref(x, adj, L1_gnn_W, L1_gnn_U), axis=-1)
    return x

_drawn_inputs = setup_inputs


def setup_inputs(seed=0):
    import zlib

    import numpy as np

    out = dict(_drawn_inputs(seed))
    spreads = {}
    factors = {}
    for name, (base, spread) in spreads.items():
        noise = np.random.default_rng([zlib.crc32(name.encode()), seed]).standard_normal(out[name].shape)
        drawn = base * np.exp(spread * noise) if base else spread * noise
        out[name] = jnp.asarray(drawn.astype(out[name].dtype))
    for name, factor in factors.items():
        out[name] = (out[name] * factor).astype(out[name].dtype)
    return out
```

```python
from contextlib import ExitStack

import concourse.bass as bass
from concourse import mybir

F32 = mybir.dt.float32
F32R = mybir.dt.float32r
BF16 = mybir.dt.bfloat16
ALU = mybir.AluOpType
ACT = mybir.ActivationFunctionType
AX = mybir.AxisListType
ds = bass.ds

P = 128
N = 4096
D = 256
FT = D // P
ROWS = 512
NB = N // ROWS
NT = N // P
TPB = ROWS // P
STEPS = 16
RAW = 4
CH = 512
NC = N // CH
HI, LO = 0, 1
EPS = 1e-5
BIG = 1e30


def is_static(v):
    return isinstance(v, int)


def convolution(nc, layer, keep, adjT, src_dram, x_rows, hT_dram, x1_dram):
    first = layer == 1
    node = keep["X"] if first else keep["H"]
    made = keep["H"] if first else keep["X"]
    W, WA, ident = keep["W"][layer], keep["WA"], keep["ident"]

    with ExitStack() as ctx:
        def sb(name, shape, dt):
            return ctx.enter_context(nc.sbuf_tensor(f"{name}{layer}", shape, dt))

        def ps(name):
            return ctx.enter_context(nc.psum_tensor(f"{name}{layer}", [P, 512], F32))

        def sem(name):
            return ctx.enter_context(nc.semaphore(f"{name}{layer}"))

        raw = sb("adj_raw", [P, RAW, 2 * ROWS], F32)
        adj = sb("adj_parts", [P, 4, 2, ROWS], F32R)
        agg = sb("agg_parts", [P, FT, 2, ROWS], F32R)
        src = sb("src_parts", [P, FT, 2, ROWS], F32R)
        src_raw = sb("src_raw", [P, FT, ROWS], F32)
        outT = sb("outT", [P, FT, ROWS], F32)
        aggP = [ps("aggP0"), ps("aggP1")]
        projP = [ps("projP0"), ps("projP1")]
        turnP = [ps("turnP0"), ps("turnP1")]

        raw_in = [sem(f"raw_in{i}_") for i in range(RAW)]
        adj_hi, adj_lo, adj_used = sem("adj_hi"), sem("adj_lo"), sem("adj_used")
        agg0_done, agg_hi, agg_lo = sem("agg0_done"), sem("agg_hi"), sem("agg_lo")
        src_in, src_hi, src_lo = sem("src_in"), sem("src_hi"), sem("src_lo")
        proj_done, turn_done = sem("proj_done"), sem("turn_done")
        outT_ready, outT_out = sem("outT_ready"), sem("outT_out")
        made_hi, made_lo = sem("made_hi"), sem("made_lo")
        if not first:
            xn = sb("x_rows", [P, 2, D], F32)
            y = sb("y", [P, 2, D], F32)
            x1 = sb("x1", [P, 2, D], F32)
            stats, mv = sb("stats", [P, 2, 6], F32), sb("mv", [P, 2, 2], F32)
            veps, rstd = sb("veps", [P, 2, 1], F32), sb("rstd", [P, 2, 1], F32)
            tick = sb("tick", [P, 1], F32)
            x_in = [sem("x_in0_"), sem("x_in1_")]
            x1_out = [sem("x1_out0_"), sem("x1_out1_")]
            y_ready, stats_ready, mv_ready = sem("y_ready"), sem("stats_ready"), sem("mv_ready")
            veps_ready, rstd_ready, x1_ready = sem("veps_ready"), sem("rstd_ready"), sem("x1_ready")
            x1T_hi, x1T_lo, att_done = sem("x1T_hi"), sem("x1T_lo"), sem("att_done")

        LAG = 1 if first else 2

        def walk(eng, step):
            for b in range(2):
                for j in range(STEPS):
                    step(b, j)
            with eng.Fori(2, NB) as b:
                for j in range(STEPS):
                    step(b, j)
            for b in range(NB, NB + LAG):
                for j in range(STEPS):
                    step(b, j)

        def live(b):
            return not is_static(b) or 0 <= b < NB

        block = ctx.enter_context(nc.Block())

        @block.sync
        def _(sp):
            def step(b, j):
                e = b - 1
                if live(b):
                    g = STEPS * b + j
                    if not is_static(b) or g >= RAW:
                        sp.wait_ge(adj_lo, 2 * (g - RAW + 1))
                    sp.dma_start(raw[:, j % RAW, :], adjT[ds(g, 1), :, :].rearrange("o p n -> (o p) n"))\
                        .then_inc(raw_in[j % RAW], 16)
                if not live(e):
                    return
                if j == 0:
                    if not is_static(e) or e >= 1:
                        sp.wait_ge(src_lo, e)
                    sp.dma_start(src_raw[:, :, :].rearrange("p f n -> p (f n)"),
                                 src_dram[ds(e, 1), :, :].rearrange("o p n -> (o p) n")).then_inc(src_in, 16)
                if not first and j in (1, 3, 5, 7):
                    k = j // 2
                    n = TPB * e + k
                    if not is_static(e) or n >= 2:
                        sp.wait_ge(y_ready, n - 1)
                    sp.dma_start(xn[:, k % 2, :], x_rows[ds(n, 1), :, :].rearrange("o p n -> (o p) n"))\
                        .then_inc(x_in[k % 2], 16)
            walk(sp, step)

        @block.gpsimd
        def _(pool):
            if first:
                return
            with pool.Fori(0, NB) as e:
                for k in range(TPB):
                    n = TPB * e + k
                    pool.wait_ge(veps_ready, n + 1)
                    nc.gpsimd.tensor_tensor(rstd[:, k % 2, :], veps[:, k % 2, :], keep["neg_half"][:, :],
                                            ALU.pow).then_inc(rstd_ready, 1)

        @block.scalar
        def _(act):
            def step(b, j):
                e = b - 1
                if live(b):
                    g = STEPS * b + j
                    act.wait_ge(raw_in[j % RAW], 16 * (STEPS // RAW * b + j // RAW + 1))
                    for t in range(2):
                        if not is_static(b) or g >= 2:
                            act.wait_ge(adj_used, 2 * g + t - 3)
                        nc.scalar.activation(adj[:, 2 * (j % 2) + t, HI, :],
                                             raw[:, j % RAW, t * ROWS:(t + 1) * ROWS],
                                             ACT.Copy).then_inc(adj_hi, 1)
                if not first and j == 2 and live(b - 2):
                    w = b - 2
                    for r in range(2):
                        act.wait_ge(att_done, 2 * w + r + 1)
                        nc.scalar.activation(made[:, ds(TPB * w + 2 * r, 2), HI, :],
                                             projP[r][:, :].rearrange("p (t n) -> p t n", t=2),
                                             ACT.Copy).then_inc(made_hi, 1)
                if not live(e):
                    return
                if j == 0:
                    for f in range(FT):
                        if f == 0:
                            act.wait_ge(agg0_done, e + 1)
                        else:
                            act.wait_ge(adj_used, 2 * STEPS * (e + 1))
                        if not is_static(e) or e >= 1:
                            act.wait_ge(proj_done, (2 if first else TPB) * e)
                        nc.scalar.activation(agg[:, f, HI, :], aggP[f][:, :], ACT.Copy).then_inc(agg_hi, 1)
                if j == 3:
                    act.wait_ge(src_in, 16 * (e + 1))
                    if not first and (not is_static(e) or e >= 1):
                        act.wait_ge(att_done, 2 * e)
                    nc.scalar.activation(src[:, :, HI, :], src_raw[:, :, :], ACT.Copy).then_inc(src_hi, 1)
                if first:
                    if j in (8, 9):
                        f = j - 8
                        act.wait_ge(proj_done, 2 * e + f + 1)
                        if not is_static(e) or e >= 1:
                            act.wait_ge(turn_done, 2 * e)
                            act.wait_ge(outT_out, 16 * e)
                        nc.scalar.activation(outT[:, f, :], projP[f][:, :], ACT.Relu).then_inc(outT_ready, 1)
                    if j == 10:
                        act.wait_ge(outT_ready, 2 * e + 2)
                        act.dma_start(hT_dram[ds(e, 1), :, :].rearrange("o p n -> (o p) n"),
                                      outT[:, :, :].rearrange("p f n -> p (f n)")).then_inc(outT_out, 16)
                    if j == 12:
                        for r in range(2):
                            act.wait_ge(turn_done, 2 * e + r + 1)
                            nc.scalar.activation(made[:, ds(TPB * e + 2 * r, 2), HI, :],
                                                 turnP[r][:, :].rearrange("p (t n) -> p t n", t=2),
                                                 ACT.Copy).then_inc(made_hi, 1)
                else:
                    if j in (7, 9, 11, 13):
                        k = (j - 7) // 2
                        n = TPB * e + k
                        act.wait_ge(x1_ready, n + 1)
                        act.dma_start(x1_dram[ds(n, 1), :, :].rearrange("o p n -> (o p) n"), x1[:, k % 2, :])\
                            .then_inc(x1_out[k % 2], 16)
                    if j == 14:
                        act.wait_ge(turn_done, TPB * e + TPB)
                        if not is_static(e) or e >= 1:
                            act.wait_ge(outT_out, 16 * e)
                            act.wait_ge(x1T_lo, e)
                        for f in range(FT):
                            nc.scalar.activation(outT[:, f, :], turnP[f][:, :], ACT.Copy).then_inc(outT_ready, 1)
                        act.wait_ge(outT_ready, 2 * e + 2)
                        act.wait_ge(proj_done, TPB * e + TPB)
                        nc.scalar.activation(src[:, :, HI, :], outT[:, :, :], ACT.Copy).then_inc(x1T_hi, 1)
                        act.dma_start(hT_dram[ds(e, 1), :, :].rearrange("o p n -> (o p) n"),
                                      outT[:, :, :].rearrange("p f n -> p (f n)")).then_inc(outT_out, 16)
            walk(act, step)
            act.wait_ge(outT_out, 16 * NB)
            if not first:
                for s in range(2):
                    act.wait_ge(x1_out[s], 16 * NT // 2)

        @block.vector
        def _(dve):
            def low(out, value, high):
                return nc.vector.tensor_tensor(out, value, high, ALU.subtract)

            def step(b, j):
                e = b - 1
                if live(b):
                    g = STEPS * b + j
                    for t in range(2):
                        dve.wait_ge(adj_hi, 2 * g + t + 1)
                        low(adj[:, 2 * (j % 2) + t, LO, :], raw[:, j % RAW, t * ROWS:(t + 1) * ROWS],
                            adj[:, 2 * (j % 2) + t, HI, :].bitcast(F32)).then_inc(adj_lo, 1)
                if not first and j == 2 and live(b - 2):
                    w = b - 2
                    for r in range(2):
                        dve.wait_ge(made_hi, 2 * w + r + 1)
                        low(made[:, ds(TPB * w + 2 * r, 2), LO, :],
                            projP[r][:, :].rearrange("p (t n) -> p t n", t=2),
                            made[:, ds(TPB * w + 2 * r, 2), HI, :].bitcast(F32)).then_inc(made_lo, 1)
                if not live(e):
                    return
                if j == 0:
                    for f in range(FT):
                        dve.wait_ge(agg_hi, 2 * e + f + 1)
                        low(agg[:, f, LO, :], aggP[f][:, :], agg[:, f, HI, :].bitcast(F32)).then_inc(agg_lo, 1)
                if j == 3:
                    dve.wait_ge(src_hi, e + 1)
                    low(src[:, :, LO, :], src_raw[:, :, :], src[:, :, HI, :].bitcast(F32)).then_inc(src_lo, 1)
                if first:
                    if j == 12:
                        for r in range(2):
                            dve.wait_ge(made_hi, 2 * e + r + 1)
                            low(made[:, ds(TPB * e + 2 * r, 2), LO, :],
                                turnP[r][:, :].rearrange("p (t n) -> p t n", t=2),
                                made[:, ds(TPB * e + 2 * r, 2), HI, :].bitcast(F32)).then_inc(made_lo, 1)
                    return
                if j in (5, 7, 9, 11):
                    k = (j - 5) // 2
                    n, s = TPB * e + k, k % 2
                    dve.wait_ge(proj_done, n + 1)
                    dve.wait_ge(x_in[s], 16 * (TPB // 2 * e + k // 2 + 1))
                    nc.vector.scalar_tensor_tensor(out=y[:, s, :], in0=projP[s][:, 0:D], scalar=0.0,
                                                   in1=xn[:, s, :], op0=ALU.max, op1=ALU.add).then_inc(y_ready, 1)
                    dve.wait_ge(y_ready, n + 1)
                    nc.vector.bn_stats(stats[:, s, :], y[:, s, :]).then_inc(stats_ready, 1)
                    dve.wait_ge(stats_ready, n + 1)
                    nc.vector.memset(tick[:, :], 0.0)
                    nc.vector.bn_aggr(mv[:, s, :], stats[:, s, :]).then_inc(mv_ready, 1)
                    dve.wait_ge(mv_ready, n + 1)
                    nc.vector.tensor_scalar_add(veps[:, s, :], mv[:, s, 1:2], EPS).then_inc(veps_ready, 1)
                if j in (6, 8, 10, 12):
                    k = (j - 6) // 2
                    n, s = TPB * e + k, k % 2
                    dve.wait_ge(rstd_ready, n + 1)
                    if not is_static(e) or n >= 2:
                        dve.wait_ge(x1_out[s], 16 * (TPB // 2 * e + k // 2))
                        dve.wait_ge(turn_done, n - 1)
                    nc.vector.tensor_scalar(x1[:, s, :], y[:, s, :], mv[:, s, 0:1], rstd[:, s, :],
                                            ALU.subtract, ALU.mult).then_inc(x1_ready, 1)
                if j == 15:
                    dve.wait_ge(x1T_hi, e + 1)
                    low(src[:, :, LO, :], outT[:, :, :], src[:, :, HI, :].bitcast(F32)).then_inc(x1T_lo, 1)
            walk(dve, step)

        @block.tensor
        def _(pe):
            def three(out, stat, mov, start, stop):
                nc.tensor.matmul(out, stat(HI), mov(HI), start=start, stop=False)
                nc.tensor.matmul(out, stat(HI), mov(LO), start=False, stop=False)
                return nc.tensor.matmul(out, stat(LO), mov(HI), start=False, stop=stop)

            def step(b, j):
                e = b - 1
                if live(b):
                    g = STEPS * b + j
                    order = [(t, f) for t in range(2) for f in range(FT)]
                    if j in (0, STEPS - 1):
                        order = [(t, f) for f in range(FT) for t in range(2)]
                    for t, f in order:
                        if f == 0:
                            pe.wait_ge(adj_lo, 2 * g + t + 1)
                        if j == 0 and t == 0 and (not is_static(b) or b >= 1):
                            pe.wait_ge(agg_lo, 2 * e + f + 1)
                        last = three(aggP[f][:, :],
                                     lambda h: node[:, 2 * j + t, h, f * P:(f + 1) * P],
                                     lambda h: adj[:, 2 * (j % 2) + t, h, :],
                                     j == 0 and t == 0, j == STEPS - 1 and t == 1)
                        if f == 1:
                            last.then_inc(adj_used, 1)
                        elif j == STEPS - 1 and t == 1:
                            last.then_inc(agg0_done, 1)
                if not live(e):
                    return
                if first:
                    if j in (5, 6):
                        o = j - 5
                        pe.wait_ge(agg_lo, 2 * e + 2)
                        pe.wait_ge(src_lo, e + 1)
                        if not is_static(e) or e >= 1:
                            pe.wait_ge(outT_ready, 2 * e - 1 + o)
                        for kt in range(2 * FT):
                            part = src if kt < FT else agg
                            last = three(projP[o][:, :], lambda h: W[:, kt, h, o * P:(o + 1) * P],
                                         lambda h: part[:, kt % FT, h, :], kt == 0, kt == 2 * FT - 1)
                        last.then_inc(proj_done, 1)
                    if j == 10:
                        for r in range(2):
                            pe.wait_ge(outT_ready, 2 * e + 2)
                            if not is_static(e) or e >= 1:
                                pe.wait_ge(made_lo, 2 * e - 1 + r)
                            for q in range(2):
                                for f in range(FT):
                                    i = 2 * r + q
                                    last = nc.tensor.transpose(turnP[r][:, q * D + f * P:q * D + (f + 1) * P],
                                                               outT[:, f, i * P:(i + 1) * P], ident[:, :])
                            last.then_inc(turn_done, 1)
                    return
                if j in (3, 5, 7, 9):
                    k = (j - 3) // 2
                    n = TPB * e + k
                    if k == 0:
                        pe.wait_ge(agg_lo, 2 * e + 2)
                        pe.wait_ge(src_lo, e + 1)
                    if k >= 2:
                        pe.wait_ge(y_ready, n - 1)
                    elif not is_static(e) or e >= 1:
                        pe.wait_ge(made_lo, 2 * e - 1 + k)
                    for kt in range(2 * FT):
                        part = src if kt < FT else agg
                        last = three(projP[k % 2][:, 0:D], lambda h: part[:, kt % FT, h, k * P:(k + 1) * P],
                                     lambda h: W[:, kt, h, :], kt == 0, kt == 2 * FT - 1)
                    last.then_inc(proj_done, 1)
                if j in (6, 8, 10, 12):
                    k = (j - 6) // 2
                    n = TPB * e + k
                    pe.wait_ge(x1_ready, n + 1)
                    if k == 0 and (not is_static(e) or e >= 1):
                        pe.wait_ge(outT_ready, 2 * e)
                    for f in range(FT):
                        last = nc.tensor.transpose(turnP[f][:, k * P:(k + 1) * P],
                                                   x1[:, k % 2, f * P:(f + 1) * P], ident[:, :])
                    last.then_inc(turn_done, 1)
                if j == 15:
                    pe.wait_ge(x1T_lo, e + 1)
                    pe.wait_ge(y_ready, TPB * e + TPB)
                    for r in range(2):
                        for q in range(2):
                            i = 2 * r + q
                            for f in range(FT):
                                last = three(projP[r][:, q * D:(q + 1) * D],
                                             lambda h: src[:, f, h, i * P:(i + 1) * P],
                                             lambda h: WA[:, f, h, :], f == 0, f == FT - 1)
                        last.then_inc(att_done, 1)
            walk(pe, step)


def setup(nc, keep, x_nodes, w1, w2, wa, waT, uT, m_dram):
    with ExitStack() as ctx:
        def sb(name, shape, dt):
            return ctx.enter_context(nc.sbuf_tensor(name, shape, dt))

        def sem(name):
            return ctx.enter_context(nc.semaphore(name))

        XS = 4
        NX = NT // XS
        w_raw = sb("w_raw", [P, 5, FT, D], F32)
        t_raw = sb("t_raw", [P, 2, FT, D], F32)
        z = sb("z", [P, FT, D], F32)
        m = sb("m", [P, FT, D], F32)
        x_raw = sb("x_raw", [P, NX, XS, D], F32)
        zP = ctx.enter_context(nc.psum_tensor("zP", [P, FT, D], F32))
        mP = ctx.enter_context(nc.psum_tensor("mP", [P, FT, D], F32))
        w_in, t_in = sem("w_in"), sem("t_in")
        x_in = [sem(f"x_chunk{i}") for i in range(NX)]
        w_hi, x_hi, z_done, z_ready, m_done, m_ready, m_out = (
            sem(n) for n in ("w_hi", "x_hi", "z_done", "z_ready", "m_done", "m_ready", "m_out"))
        zeroed, done = sem("zeroed"), sem("setup_done")
        W1, W2, WA, X = keep["W"][1], keep["W"][2], keep["WA"], keep["X"]
        block = ctx.enter_context(nc.Block())

        @block.sync
        def _(sp):
            for i in range(NX):
                sp.dma_start(x_raw[:, i, :, :], x_nodes[:, i * XS:(i + 1) * XS, :]).then_inc(x_in[i], 16)

        @block.gpsimd
        def _(pool):
            nc.gpsimd.memset(keep["ident"][:, :], 0.0).then_inc(zeroed, 1)
            nc.gpsimd.memset(keep["neg_half"][:, :], -0.5).then_inc(done, 1)
            pool.wait_ge(zeroed, 1)
            nc.gpsimd.affine_select(out=keep["ident"][:, :], in_=keep["ident"][:, :], compare_op=ALU.not_equal,
                                    fill=1.0, base=0, pattern=[[-1, P]], channel_multiplier=1).then_inc(done, 1)

        @block.scalar
        def _(act):
            act.dma_start(t_raw[:, 0, :, :], waT).then_inc(t_in, 16)
            act.dma_start(t_raw[:, 1, :, :], uT).then_inc(t_in, 16)
            act.dma_start(w_raw[:, 0:2, :, :].rearrange("p a f n -> p (a f) n"), w1).then_inc(w_in, 16)
            act.dma_start(w_raw[:, 2:4, :, :].rearrange("p a f n -> p (a f) n"), w2).then_inc(w_in, 16)
            act.dma_start(w_raw[:, 4, :, :], wa).then_inc(w_in, 16)
            act.wait_ge(w_in, 48)
            nc.scalar.activation(W1[:, :, HI, :], w_raw[:, 0:2, :, :].rearrange("p a f n -> p (a f) n"),
                                 ACT.Copy).then_inc(w_hi, 1)
            nc.scalar.activation(W2[:, :, HI, :], w_raw[:, 2:4, :, :].rearrange("p a f n -> p (a f) n"),
                                 ACT.Copy).then_inc(w_hi, 1)
            nc.scalar.activation(WA[:, :, HI, :], w_raw[:, 4, :, :], ACT.Copy).then_inc(w_hi, 1)
            for i in range(NX):
                act.wait_ge(x_in[i], 16)
                nc.scalar.activation(X[:, i * XS:(i + 1) * XS, HI, :], x_raw[:, i, :, :],
                                     ACT.Copy).then_inc(x_hi, 1)
            act.wait_ge(m_done, 1)
            nc.scalar.activation(m[:, :, :], mP[:, :, :], ACT.Copy).then_inc(m_ready, 1)
            act.wait_ge(m_ready, 1)
            act.dma_start(m_dram, m[:, :, :]).then_inc(m_out, 16)
            act.wait_ge(m_out, 16)

        @block.vector
        def _(dve):
            sub = ALU.subtract
            dve.wait_ge(z_done, 1)
            nc.vector.tensor_copy(z[:, :, :], zP[:, :, :]).then_inc(z_ready, 1)
            dve.wait_ge(w_hi, 3)
            for out, value in ((W1, w_raw[:, 0:2, :, :].rearrange("p a f n -> p (a f) n")),
                               (W2, w_raw[:, 2:4, :, :].rearrange("p a f n -> p (a f) n")),
                               (WA, w_raw[:, 4, :, :])):
                nc.vector.tensor_tensor(out[:, :, LO, :], value, out[:, :, HI, :].bitcast(F32), sub)\
                    .then_inc(done, 1)
            for i in range(NX):
                dve.wait_ge(x_hi, i + 1)
                at = slice(i * XS, (i + 1) * XS)
                nc.vector.tensor_tensor(X[:, at, LO, :], x_raw[:, i, :, :], X[:, at, HI, :].bitcast(F32), sub)\
                    .then_inc(done, 1)

        @block.tensor
        def _(pe):
            pe.wait_ge(t_in, 32)
            for o in range(FT):
                for k in range(FT):
                    last = nc.tensor.matmul(zP[:, o, :], t_raw[:, 1, k, o * P:(o + 1) * P], t_raw[:, 0, k, :],
                                            start=k == 0, stop=k == FT - 1)
            last.then_inc(z_done, 1)
            pe.wait_ge(z_ready, 1)
            for o in range(FT):
                for k in range(FT):
                    last = nc.tensor.matmul(mP[:, o, :], t_raw[:, 0, k, o * P:(o + 1) * P], z[:, k, :],
                                            start=k == 0, stop=k == FT - 1)
            last.then_inc(m_done, 1)


def attention(nc, keep, adj_dram, x1T_dram, x1_dram, m_dram, out):
    H, XT = keep["X"], keep["H"].rearrange("p t h n -> p (t h n)").rearrange("p (f h n) -> p f h n", f=FT, h=2)
    ident = keep["ident"]
    SLOTS = 16
    BODY = 16
    LAST = NT * NC

    with ExitStack() as ctx:
        def sb(name, shape, dt):
            return ctx.enter_context(nc.sbuf_tensor(name, shape, dt))

        def ps(name, shape=(P, 512)):
            return ctx.enter_context(nc.psum_tensor(name, list(shape), F32))

        def sem(name):
            return ctx.enter_context(nc.semaphore(name))

        adj = sb("adj", [P, SLOTS, CH], F32)
        pm = sb("pm", [P, NC + 1, CH], F32)
        bias = sb("bias", [P, 2, CH], BF16)
        turned = sb("turned", [P, 2, 2, CH], F32R)
        M = sb("score_m", [P, FT, 2, D], F32R)
        strip = sb("strip", [P, (2 * NC - 1) * P], BF16)
        q = sb("q", [P, FT, 2, 2 * P], F32R)
        mx, sums = sb("mx", [P, 2, NC], F32), sb("sums", [P, 2, NC], F32)
        mrow, nmax = sb("mrow", [P, 2, 1], F32), sb("nmax", [P, 2, 1], F32)
        rsum, rinv = sb("rsum", [P, 2, 1], F32), sb("rinv", [P, 2, 1], F32)
        tick = sb("tick_att", [P, 1], F32)
        cross = sb("cross", [P, D], F32)
        both = sb("both", [P, D], F32)
        x1 = sb("x1_rows", [P, 2, D], F32)
        y = sb("y_att", [P, D], F32)
        fin = sb("fin", [P, 2, D], F32)
        stats, mv = sb("stats_att", [P, 2, 6], F32), sb("mv_att", [P, 2, 2], F32)
        veps, rstd = sb("veps_att", [P, 2, 1], F32), sb("rstd_att", [P, 2, 1], F32)
        scoreP = [ps(f"scoreP{i}") for i in range(4)]
        turnP = [ps("turn_att0"), ps("turn_att1")]
        accP = ps("accP")
        qP = ps("qP", (P, FT, 2 * P))

        adj_in = [sem(f"adj_in{i}") for i in range(SLOTS // 2)]
        xt_in = [sem(f"xt_in{i}") for i in range(4)]
        x1_in = [sem("x1_in0"), sem("x1_in1")]
        out_sent = [sem("out_sent0"), sem("out_sent1")]
        xt_hi, xt_lo = sem("xt_hi"), sem("xt_lo")
        m_in, m_hi, m_lo, zeroed, strip_ready = (sem(n) for n in ("m_in", "m_hi", "m_lo", "zeroed_strip", "strip_ready"))
        m_raw = pm[:, 0, :].rearrange("p (f n) -> p f n", f=FT)
        q_done, q_hi, q_lo = sem("q_done"), sem("q_hi"), sem("q_lo")
        diag_added, bias_ready = sem("diag_added"), sem("bias_ready")
        scores_done, masked, mrow_ready, nmax_ready = (sem(n) for n in
                                                       ("scores_done", "masked", "mrow_ready", "nmax_ready"))
        exp_done, weighted, turn_done = sem("exp_done"), sem("weighted"), sem("turn_att_done")
        turned_hi, turned_lo, av_done = sem("turned_hi"), sem("turned_lo"), sem("av_done")
        cross_ready, acc_read, rsum_ready, rinv_ready = (sem(n) for n in
                                                         ("cross_ready", "acc_read", "rsum_ready", "rinv_ready"))
        y_ready, stats_ready, mv_ready = sem("y_att_ready"), sem("stats_att_ready"), sem("mv_att_ready")
        veps_ready, rstd_ready, fin_ready = sem("veps_att_ready"), sem("rstd_att_ready"), sem("fin_ready")

        def slot(a):
            return NC if a == 2 * NC - 1 else a % NC

        def walk(eng, step, tail=BODY + 2):
            for s in range(BODY):
                step(0, s)
            with eng.Fori(1, NT // 2 - 1) as k:
                for s in range(BODY):
                    step(k, s)
            for s in range(BODY + tail):
                step(NT // 2 - 1 + s // BODY, s % BODY)

        def live(k, s, back):
            return not is_static(k) or 0 <= BODY * k + s - back < LAST

        block = ctx.enter_context(nc.Block())

        @block.sync
        def _(sp):
            def adj_load(k, s8):
                w = SLOTS // 2 * k + s8
                sp.dma_start(adj[:, 2 * s8:2 * s8 + 2, :].rearrange("p c n -> p (c n)"),
                             adj_dram[ds(w, 1), :, :].rearrange("o p n -> (o p) n")).then_inc(adj_in[s8], 16)

            def x1_load(n, s):
                sp.dma_start(x1[:, s, :], x1_dram[ds(n, 1), :, :].rearrange("o p n -> (o p) n"))\
                    .then_inc(x1_in[s], 16)

            def stage(c):
                r = c % 4
                sp.dma_start(adj[:, 8 + 2 * r:10 + 2 * r, :], x1T_dram[c, :, :]
                             .rearrange("p (f n) -> p f n", f=FT)).then_inc(xt_in[r], 16)

            sp.dma_start(m_raw, m_dram).then_inc(m_in, 16)
            stage(0)
            stage(1)
            for s8 in range(4):
                adj_load(0, s8)
                if s8 < 2:
                    stage(2 + s8)
            for c in range(4, NC):
                sp.wait_ge(xt_lo, c - 3)
                stage(c)
            for n in range(2):
                x1_load(n, n)
            for s8 in range(4, 8):
                sp.wait_ge(xt_lo, s8 + 1)
                adj_load(0, s8)

            def store(n, s):
                sp.wait_ge(fin_ready, n + 1)
                sp.dma_start(out[ds(n, 1), :, :].rearrange("o p n -> (o p) n"), fin[:, s, :])\
                    .then_inc(out_sent[s], 16)

            def turnover(n, u):
                store(n, u)
                sp.wait_ge(y_ready, n + 1)
                x1_load(n + 2, u)

            def pair(k):
                for s8 in range(8):
                    sp.wait_ge(weighted, 16 * k + 2 * s8 - 14)
                    adj_load(k, s8)
                    if s8 == 3 and (not is_static(k) or k >= 2):
                        turnover(2 * k - 3, 1)
                    if s8 == 7:
                        turnover(2 * k - 2, 0)

            pair(1)
            with sp.Fori(2, NT // 2) as k:
                pair(k)
            turnover(NT - 3, 1)
            store(NT - 2, 0)
            store(NT - 1, 1)
            for s in range(2):
                sp.wait_ge(out_sent[s], 16 * NT // 2)

        @block.gpsimd
        def _(pool):
            def diag(k, s, ahead):
                p, s = k + (s + ahead) // BODY, (s + ahead) % BODY
                u, c = s // NC, s % NC
                pool.wait_ge(adj_in[s // 2], 16 * (p + 1))
                col = s * CH + (p % 2) * (2 * P) + u * P
                off = (NC - 1 - c) * P + (p // 2) * P
                at = adj[:, :, :].rearrange("p c n -> p (c n)")[:, ds(col, P)]
                nc.gpsimd.tensor_tensor(at, at, strip[:, ds(off, P)], ALU.add).then_inc(diag_added, 1)

            def step(k, s):
                if live(k, s, 8):
                    t = BODY * k + s - 8
                    a = (s - 8) % BODY
                    pool.wait_ge(exp_done, t + 1)
                    nc.gpsimd.tensor_tensor(pm[:, slot(a), :], pm[:, slot(a), :], adj[:, a, :], ALU.mult)\
                        .then_inc(weighted, 1)
                if live(k, s, -4):
                    diag(k, s, 4)
                if s % NC == 4 and (not is_static(k) or 0 <= 2 * k + s // NC - 2 < NT):
                    n = 2 * k + s // NC - 2
                    r = s // NC
                    pool.wait_ge(veps_ready, n + 1)
                    nc.gpsimd.tensor_tensor(rstd[:, r, :], veps[:, r, :], keep["neg_half"][:, :], ALU.pow)\
                        .then_inc(rstd_ready, 1)

            nc.gpsimd.memset(strip[:, :], 0.0).then_inc(zeroed, 1)
            pool.wait_ge(zeroed, 1)
            mid = strip[:, (NC - 1) * P:NC * P]
            nc.gpsimd.affine_select(out=mid, in_=mid, compare_op=ALU.not_equal, fill=1.0, base=0,
                                    pattern=[[-1, P]], channel_multiplier=1).then_inc(strip_ready, 1)
            pool.wait_ge(strip_ready, 1)
            for s in range(4):
                diag(0, s, 0)
            walk(pool, step)

        @block.scalar
        def _(act):
            def xt_high(c):
                act.wait_ge(xt_in[c % 4], 16 * (c // 4 + 1))
                nc.scalar.activation(XT[:, :, HI, c * CH:(c + 1) * CH],
                                     adj[:, 8 + 2 * (c % 4):10 + 2 * (c % 4), :], ACT.Copy).then_inc(xt_hi, 1)

            def q_high(pair, u):
                act.wait_ge(q_done, pair + 1)
                at = slice(u * P, (u + 1) * P)
                nc.scalar.activation(q[:, :, HI, at], qP[:, :, at], ACT.Copy).then_inc(q_hi, 1)

            def step(k, s):
                if is_static(k) and k == 0 and s + 2 < NC:
                    xt_high(s + 2)
                if s == 12 and (not is_static(k) or k + 1 < NT // 2):
                    act.wait_ge(scores_done, BODY * k + NC)
                    q_high(k + 1, 0)
                if s == 1 and (not is_static(k) or 1 <= k < NT // 2):
                    act.wait_ge(scores_done, BODY * k)
                    q_high(k, 1)
                if live(k, s, 8):
                    t, a = BODY * k + s - 8, (s - 8) % BODY
                    u, c = a // NC, a % NC
                    if c == 0:
                        m = 2 * k + (s - 8) // NC
                        act.wait_ge(nmax_ready, m + 1)
                    nc.scalar.activation(pm[:, slot(a), :], pm[:, slot(a), :], ACT.Exp, bias=nmax[:, u, :],
                                         accum_out=sums[:, u, c:c + 1]).then_inc(exp_done, 1)
                if live(k, s, 9):
                    t, c = BODY * k + s - 9, (s - 9) % NC
                    act.wait_ge(turn_done, t + 1)
                    if not is_static(k) or t >= 2:
                        act.wait_ge(av_done, t - 1)
                    nc.scalar.activation(turned[:, c % 2, HI, :], turnP[c % 2][:, :], ACT.Copy)\
                        .then_inc(turned_hi, 1)
                if s % NC == 1 and (not is_static(k) or 0 <= 2 * k + s // NC - 2 < NT):
                    n = 2 * k + s // NC - 2
                    act.wait_ge(av_done, NC * n + NC)
                    if not is_static(k) or n >= 1:
                        act.wait_ge(acc_read, n)
                    nc.scalar.activation(cross[:, :], accP[:, D:2 * D], ACT.Copy).then_inc(cross_ready, 1)

            act.wait_ge(m_in, 16)
            nc.scalar.activation(M[:, :, HI, :], m_raw, ACT.Copy).then_inc(m_hi, 1)
            xt_high(0)
            q_high(0, 0)
            q_high(0, 1)
            xt_high(1)
            walk(act, step)

        @block.vector
        def _(dve):
            def low(out, value, high):
                return nc.vector.tensor_tensor(out, value, high, ALU.subtract)

            def xt_low(c):
                dve.wait_ge(xt_hi, c + 1)
                low(XT[:, :, LO, c * CH:(c + 1) * CH], adj[:, 8 + 2 * (c % 4):10 + 2 * (c % 4), :],
                    XT[:, :, HI, c * CH:(c + 1) * CH].bitcast(F32)).then_inc(xt_lo, 1)

            def q_low(pair, u):
                dve.wait_ge(q_hi, 2 if is_static(pair) and pair == 0 else 2 * pair + u + 1)
                at = slice(u * P, (u + 1) * P)
                low(q[:, :, LO, at], qP[:, :, at], q[:, :, HI, at].bitcast(F32)).then_inc(q_lo, 1)

            def mask_bias(k, s, ahead):
                t, a = BODY * k + s + ahead, (s + ahead) % BODY
                if not is_static(k) or t >= 2:
                    dve.wait_ge(masked, t - 1)
                dve.wait_ge(diag_added, t + 1)
                nc.vector.tensor_scalar(bias[:, a % 2, :], adj[:, a, :], 0.0, -BIG, ALU.is_le, ALU.mult)\
                    .then_inc(bias_ready, 1)

            def step(k, s):
                if is_static(k) and k == 0 and s + 2 < NC:
                    xt_low(s + 2)
                if live(k, s, 9):
                    t, c = BODY * k + s - 9, (s - 9) % NC
                    dve.wait_ge(turned_hi, t + 1)
                    low(turned[:, c % 2, LO, :], turnP[c % 2][:, :], turned[:, c % 2, HI, :].bitcast(F32))\
                        .then_inc(turned_lo, 1)
                if s % NC == 1 and (not is_static(k) or 0 <= 2 * k + s // NC - 2 < NT):
                    n = 2 * k + s // NC - 2
                    dve.wait_ge(cross_ready, n + 1)
                    if not is_static(k) or n >= 1:
                        dve.wait_ge(y_ready, n)
                    nc.vector.tensor_tensor(both[:, :], accP[:, 0:D], cross[:, :], ALU.add).then_inc(acc_read, 1)
                if live(k, s, 0):
                    t, u, c = BODY * k + s, s // NC, s % NC
                    dve.wait_ge(scores_done, t + 1)
                    dve.wait_ge(bias_ready, t + 1)
                    if is_static(k) and t == 0:
                        dve.wait_ge(m_lo, 1)
                    back = 2 * NC if c == NC - 1 else NC
                    if not is_static(k) or t >= back:
                        dve.wait_ge(turn_done, t - back + 1)
                    if not is_static(k) or t >= 1:
                        dve.wait_ge(masked, t)
                    nc.vector.memset(tick[:, :], 0.0)
                    nc.vector.tensor_tensor_reduce(out=pm[:, slot(s), :], in0=scoreP[s % 4][:, :], in1=bias[:, s % 2, :],
                                                   scale=1.0, scalar=-2.0 * BIG, op0=ALU.add, op1=ALU.max,
                                                   accum_out=mx[:, u, c:c + 1]).then_inc(masked, 1)
                    if c == NC - 1:
                        m = 2 * k + u
                        dve.wait_ge(masked, t + 1)
                        nc.vector.reduce_max(mrow[:, u, :], mx[:, u, :], AX.X).then_inc(mrow_ready, 1)
                        dve.wait_ge(mrow_ready, m + 1)
                        nc.vector.tensor_scalar_mul(nmax[:, u, :], mrow[:, u, :], -1.0).then_inc(nmax_ready, 1)
                if live(k, s, -1):
                    mask_bias(k, s, 1)
                if s == 12 and (not is_static(k) or k + 1 < NT // 2):
                    q_low(k + 1, 0)
                if s == 1 and (not is_static(k) or 1 <= k < NT // 2):
                    q_low(k, 1)
                if s % NC == 2 and (not is_static(k) or 0 <= 2 * k + s // NC - 2 < NT):
                    n, r = 2 * k + s // NC - 2, s // NC
                    nc.vector.reduce_sum(rsum[:, r, :], sums[:, r, :], AX.X).then_inc(rsum_ready, 1)
                    dve.wait_ge(rsum_ready, n + 1)
                    nc.vector.reciprocal(rinv[:, r, :], rsum[:, r, :]).then_inc(rinv_ready, 1)
                    dve.wait_ge(rinv_ready, n + 1)
                    dve.wait_ge(acc_read, n + 1)
                    dve.wait_ge(x1_in[r], 16 * k)
                    nc.vector.scalar_tensor_tensor(out=y[:, :], in0=both[:, :], scalar=rinv[:, r, :],
                                                   in1=x1[:, r, :], op0=ALU.mult, op1=ALU.add).then_inc(y_ready, 1)
                if s % NC == 3 and (not is_static(k) or 0 <= 2 * k + s // NC - 2 < NT):
                    n, r = 2 * k + s // NC - 2, s // NC
                    dve.wait_ge(y_ready, n + 1)
                    nc.vector.bn_stats(stats[:, r, :], y[:, :]).then_inc(stats_ready, 1)
                    dve.wait_ge(stats_ready, n + 1)
                    nc.vector.memset(tick[:, :], 0.0)
                    nc.vector.bn_aggr(mv[:, r, :], stats[:, r, :]).then_inc(mv_ready, 1)
                    dve.wait_ge(mv_ready, n + 1)
                    nc.vector.tensor_scalar_add(veps[:, r, :], mv[:, r, 1:2], EPS).then_inc(veps_ready, 1)
                if s % NC == 6 and (not is_static(k) or 0 <= 2 * k + s // NC - 2 < NT):
                    n, r = 2 * k + s // NC - 2, s // NC
                    dve.wait_ge(rstd_ready, n + 1)
                    if not is_static(k) or n >= 2:
                        dve.wait_ge(out_sent[r], 16 * (k - 1))
                    nc.vector.tensor_scalar(fin[:, r, :], y[:, :], mv[:, r, 0:1], rstd[:, r, :],
                                            ALU.subtract, ALU.mult).then_inc(fin_ready, 1)

            dve.wait_ge(m_hi, 1)
            low(M[:, :, LO, :], m_raw, M[:, :, HI, :].bitcast(F32)).then_inc(m_lo, 1)
            xt_low(0)
            q_low(0, 0)
            q_low(0, 1)
            xt_low(1)
            mask_bias(0, 0, 0)
            walk(dve, step)

        @block.tensor
        def _(pe):
            def three(out, stat, mov, start, stop):
                nc.tensor.matmul(out, stat(HI), mov(HI), start=start, stop=False)
                nc.tensor.matmul(out, stat(HI), mov(LO), start=False, stop=False)
                return nc.tensor.matmul(out, stat(LO), mov(HI), start=False, stop=stop)

            def q_pair(pair):
                for o in range(FT):
                    for f in range(FT):
                        last = three(qP[:, o, :], lambda h: M[:, f, h, o * P:(o + 1) * P],
                                     lambda h: XT[:, f, h, ds(2 * P * pair, 2 * P)], f == 0, f == FT - 1)
                last.then_inc(q_done, 1)

            def step(k, s):
                if live(k, s, 0):
                    t, u, c = BODY * k + s, s // NC, s % NC
                    if s == 0 or s == NC:
                        pe.wait_ge(q_lo, 2 * k + u + 1)
                    if is_static(k) and k == 0 and s < NC:
                        pe.wait_ge(xt_lo, s + 1)
                    if not is_static(k) or t >= 4:
                        pe.wait_ge(masked, t - 3)
                    for f in range(FT):
                        last = three(scoreP[s % 4][:, :], lambda h: q[:, f, h, u * P:(u + 1) * P],
                                     lambda h: XT[:, f, h, c * CH:(c + 1) * CH], f == 0, f == FT - 1)
                    last.then_inc(scores_done, 1)
                if s == 10 and (not is_static(k) or k + 1 < NT // 2):
                    pe.wait_ge(q_lo, 2 * k + 2)
                    q_pair(k + 1)
                if live(k, s, 9):
                    t, a = BODY * k + s - 9, (s - 9) % BODY
                    c = a % NC
                    pe.wait_ge(weighted, t + 1)
                    if not is_static(k) or t >= 2:
                        pe.wait_ge(turned_lo, t - 1)
                    for i in range(CH // P):
                        last = nc.tensor.transpose(turnP[c % 2][:, i * P:(i + 1) * P],
                                                   pm[:, slot(a), i * P:(i + 1) * P], ident[:, :])
                    last.then_inc(turn_done, 1)
                if live(k, s, 10):
                    t, c = BODY * k + s - 10, (s - 10) % NC
                    pe.wait_ge(turned_lo, t + 1)
                    if c == 0:
                        m = 2 * k + (s - 10) // NC
                        if not is_static(k) or m >= 1:
                            pe.wait_ge(acc_read, m)
                    for i in range(CH // P):
                        j = c * (CH // P) + i
                        at = slice(i * P, (i + 1) * P)
                        nc.tensor.matmul(accP[:, :], turned[:, c % 2, HI, at],
                                         H[:, j, :, :].rearrange("p h n -> p (h n)"),
                                         start=j == 0, stop=False)
                        last = nc.tensor.matmul(accP[:, 0:D], turned[:, c % 2, LO, at], H[:, j, HI, :],
                                                start=False, stop=j == NT - 1)
                    last.then_inc(av_done, 1)

            pe.wait_ge(m_lo, 1)
            pe.wait_ge(xt_lo, 1)
            q_pair(0)
            walk(pe, step)


def build(nc, x_nodes, x_rows, xT, adjT, adjN, w1, w2, wa, waT, uT, out):
    h1T = nc.dram_tensor("h1T", (NB, P, FT * ROWS), F32, kind="Internal").ap()
    x1T = nc.dram_tensor("x1T", (NB, P, FT * ROWS), F32, kind="Internal").ap()
    x1 = nc.dram_tensor("x1d", (NT, P, D), F32, kind="Internal").ap()
    m = nc.dram_tensor("md", (P, FT, D), F32, kind="Internal").ap()
    with ExitStack() as ctx:
        def sb(where, name, shape, dt):
            return where.enter_context(nc.sbuf_tensor(name, shape, dt))

        keep = {
            "X": sb(ctx, "node_x", [P, NT, 2, D], F32R),
            "H": sb(ctx, "node_h", [P, NT, 2, D], F32R),
            "ident": sb(ctx, "ident", [P, P], F32),
            "neg_half": sb(ctx, "neg_half", [P, 1], F32),
        }
        with ExitStack() as both:
            keep["WA"] = sb(both, "wa_parts", [P, FT, 2, D], F32R)
            keep["W"] = {2: sb(both, "w2_parts", [P, 2 * FT, 2, D], F32R)}
            with ExitStack() as one:
                keep["W"][1] = sb(one, "w1_parts", [P, 2 * FT, 2, D], F32R)
                setup(nc, keep, x_nodes, w1, w2, wa, waT, uT, m)
                convolution(nc, 1, keep, adjT, xT, None, h1T, None)
            convolution(nc, 2, keep, adjT, h1T, x_rows, x1T, x1)
        attention(nc, keep, adjN, x1T, x1, m, out)


def kernel(x, adj, L0_gnn_W1, L0_gnn_W2, L1_gnn_W, L1_gnn_U):
    import numpy as np
    import concourse.bacc as bacc
    from concourse.bass_utils import run_bass_kernel_spmd

    x, adj = np.asarray(x), np.asarray(adj)
    tiles = lambda w: np.ascontiguousarray(np.asarray(w).reshape(-1, P, D).transpose(1, 0, 2))
    arrays = {
        "x_nodes": tiles(x),
        "x_rows": x.reshape(NT, P, D),
        "xT": np.ascontiguousarray(x.reshape(NB, ROWS, FT, P).transpose(0, 3, 2, 1)).reshape(NB, P, FT * ROWS),
        "adjT": np.ascontiguousarray(adj.reshape(NB, ROWS, STEPS, 2, P).transpose(0, 2, 4, 3, 1))
        .reshape(NB * STEPS, P, 2 * ROWS),
        "adjN": np.ascontiguousarray(adj.reshape(NT, P, NC // 2, 2 * CH).transpose(0, 2, 1, 3))
        .reshape(NT * NC // 2, P, 2 * CH),
        "w1": tiles(L0_gnn_W1),
        "w2": tiles(L0_gnn_W2),
        "wa": tiles(L1_gnn_W),
        "waT": tiles(np.asarray(L1_gnn_W).T),
        "uT": tiles(np.asarray(L1_gnn_U).T),
    }
    nc = bacc.Bacc("TRN2", target_bir_lowering=False, num_devices=1)
    args = [nc.dram_tensor(n, a.shape, mybir.dt.from_np(a.dtype), kind="ExternalInput").ap()
            for n, a in arrays.items()]
    out = nc.dram_tensor("out", (NT, P, D), F32, kind="ExternalOutput").ap()
    build(nc, *args, out)
    r = run_bass_kernel_spmd(nc, [arrays], core_ids=[0])
    return r.results[0]["out"].reshape(N, D)
```

```python
from contextlib import ExitStack

import concourse.bass as bass
from concourse import mybir

F32 = mybir.dt.float32
F32R = mybir.dt.float32r
BF16 = mybir.dt.bfloat16
ALU = mybir.AluOpType
ACT = mybir.ActivationFunctionType
AX = mybir.AxisListType
ds = bass.ds

P = 128
N = 4096
D = 256
FT = D // P
ROWS = 512
NB = N // ROWS
NT = N // P
TPB = ROWS // P
STEPS = 16
RAW = 4
CH = 512
NC = N // CH
EARLY = 7
HI, LO = 0, 1
EPS = 1e-5
BIG = 1e30


def is_static(v):
    return isinstance(v, int)


def x1T_view(keep):
    return keep["H"].rearrange("p t h n -> p (t h n)").rearrange("p (f h n) -> p f h n", f=FT, h=2)


def convolutions(nc, keep, adjT, xT, x_nodes, x_rows, w1, w2, wa, waT, uT, h1T_dram, x1T_dram, x1_dram):
    X, H, WA, M, ident = (keep[n] for n in ("X", "H", "WA", "M", "ident"))
    XT = x1T_view(keep)
    XS = 4
    NX = NT // XS

    with ExitStack() as ctx:
        def sb(name, shape, dt):
            return ctx.enter_context(nc.sbuf_tensor(name, shape, dt))

        def ps(name):
            return ctx.enter_context(nc.psum_tensor(name, [P, 512], F32))

        def sem(name):
            return ctx.enter_context(nc.semaphore(name))

        raw = sb("adj_raw", [P, RAW, 2 * ROWS], F32)
        adj = sb("adj_parts", [P, 4, 2, ROWS], F32R)
        agg = sb("agg_parts", [P, FT, 2, ROWS], F32R)
        src = sb("src_parts", [P, FT, 2, ROWS], F32R)
        src_raw = sb("src_raw", [P, FT, ROWS], F32)
        outT = sb("outT", [P, FT, ROWS], F32)
        W = sb("w_parts", [P, 2 * FT, 2, D], F32R)
        rows = sb("rows", [P, 3, 2, D], F32)
        xn, y, x1 = (rows[:, i, :, :] for i in range(3))
        stats, mv = sb("stats", [P, 2, 6], F32), sb("mv", [P, 2, 2], F32)
        veps, rstd = sb("veps", [P, 2, 1], F32), sb("rstd", [P, 2, 1], F32)
        tick = sb("tick", [P, 1], F32)
        aggP = [ps("aggP0"), ps("aggP1")]
        projP = [ps("projP0"), ps("projP1")]
        turnP = [ps("turnP0"), ps("turnP1")]

        as_tiles = lambda buf: buf.rearrange("p f n -> p (f n)").rearrange("p (k n) -> p k n", n=D)
        x_raw = [as_tiles(src_raw[:, :, :]), as_tiles(outT[:, :, :])]
        waT_raw, uT_raw, z = xn, y, x1
        w1_raw, wa_raw = rows[:, 0:2, :, :].rearrange("p a k n -> p (a k) n"), x1
        w2_raw = as_tiles(src_raw[:, :, :])
        zP, mP = (projP[i][:, :].rearrange("p (f n) -> p f n", f=FT) for i in range(2))

        raw_in = [sem(f"raw_in{i}") for i in range(RAW)]
        adj_hi, adj_lo, adj_used = sem("adj_hi"), sem("adj_lo"), sem("adj_used")
        agg0_done, agg_hi, agg_lo = sem("agg0_done"), sem("agg_hi"), sem("agg_lo")
        ident_zeroed, constants = sem("ident_zeroed"), sem("constants")
        x_in = [sem("x_in0"), sem("x_in1")]
        x_hi, x_lo = sem("x_hi"), sem("x_lo")
        w_in, w_hi, w_lo = sem("w_in"), sem("w_hi"), sem("w_lo")
        wa_in, wa_hi, wa_lo = sem("wa_in"), sem("wa_hi"), sem("wa_lo")
        t_in, z_done, z_ready = sem("t_in"), sem("z_done"), sem("z_ready")
        m_done, m_hi, m_lo = sem("m_done"), sem("m_hi"), sem("m_lo")
        src_in, src_hi, src_lo, proj_done, turn_done, outT_ready, outT_out, made_hi, made_lo = (
            {layer: sem(f"{name}_l{layer}") for layer in (1, 2)} for name in
            ("src_in", "src_hi", "src_lo", "proj_done", "turn_done", "outT_ready", "outT_out", "made_hi", "made_lo"))
        rows_in = [sem("rows_in0"), sem("rows_in1")]
        x1_out = [sem("x1_out0"), sem("x1_out1")]
        y_ready, stats_ready, mv_ready = sem("y_ready"), sem("stats_ready"), sem("mv_ready")
        veps_ready, rstd_ready, x1_ready = sem("veps_ready"), sem("rstd_ready"), sem("x1_ready")
        x1T_hi, x1T_lo, att_done = sem("x1T_hi"), sem("x1T_lo"), sem("att_done")
        xt_in = [sem(f"xt_early{i}") for i in range(RAW)]
        xt_hi, xt_lo = sem("xt_early_hi"), sem("xt_early_lo")
        EARLY_AT = (4, 6, 8, 10, 12, 14, 15)

        def walk(eng, stream, epilogue1, epilogue2):
            for b in range(2):
                for j in range(STEPS):
                    stream(1, b, j)
                    if b >= 1:
                        epilogue1(b - 1, j)
            with eng.Fori(2, NB) as b:
                for j in range(STEPS):
                    stream(1, b, j)
                    epilogue1(b - 1, j)
            for j in range(STEPS):
                stream(2, 0, j)
                epilogue1(NB - 1, j)
            for j in range(STEPS):
                stream(2, 1, j)
                epilogue2(0, j)
            with eng.Fori(2, NB) as b:
                for j in range(STEPS):
                    stream(2, b, j)
                    epilogue2(b - 1, j)
            for e in (NB - 1, NB):
                for j in range(STEPS):
                    epilogue2(e, j)

        def whole(layer, b):
            return NB * (layer - 1) + b

        def later(e, first=1):
            return not is_static(e) or e >= first

        block = ctx.enter_context(nc.Block())

        @block.sync
        def _(sp):
            def load(out, dram, n):
                return sp.dma_start(out, dram[ds(n, 1), :, :].rearrange("o p n -> (o p) n"))

            def stream(layer, b, j):
                g = STEPS * whole(layer, b) + j
                start = layer == 1 and is_static(b) and b == 0
                if start and j % 2 == 0:
                    i = j // 2
                    if i >= 2:
                        sp.wait_ge(x_lo, i - 1)
                    sp.dma_start(x_raw[i % 2], x_nodes[:, i * XS:(i + 1) * XS, :]).then_inc(x_in[i % 2], 16)
                if not (layer == 1 and is_static(b) and g < RAW):
                    sp.wait_ge(adj_lo, 2 * (g - RAW + 1))
                load(raw[:, j % RAW, :], adjT, STEPS * b + j).then_inc(raw_in[j % RAW], 16)
                if start and j == 2:
                    sp.dma_start(waT_raw, waT).then_inc(t_in, 16)
                    sp.dma_start(uT_raw, uT).then_inc(t_in, 16)
                if start and j == 9:
                    sp.wait_ge(m_done, 1)
                    sp.dma_start(w1_raw, w1).then_inc(w_in, 16)
                    sp.dma_start(wa_raw, wa).then_inc(wa_in, 16)

            def source(layer, dram, e):
                if later(e):
                    sp.wait_ge(src_lo[layer], e)
                load(src_raw[:, :, :].rearrange("p f n -> p (f n)"), dram, e).then_inc(src_in[layer], 16)

            def epilogue1(e, j):
                if j == 0:
                    source(1, xT, e)
                if is_static(e) and e == NB - 1 and j == 8:
                    sp.wait_ge(src_lo[1], NB)
                    sp.dma_start(w2_raw, w2).then_inc(w_in, 16)

            def early(c):
                sp.wait_ge(outT_out[2], 16 * (c + 1))
                if c < RAW:
                    sp.wait_ge(adj_lo, 4 * STEPS * NB - 2 * (RAW - 1 - c))
                else:
                    sp.wait_ge(xt_lo, c - RAW + 1)
                load(raw[:, c % RAW, :], x1T_dram, c).then_inc(xt_in[c % RAW], 16)

            def epilogue2(e, j):
                if is_static(e) and e == NB:
                    return
                if is_static(e) and e == 0 and j == 2:
                    sp.wait_ge(w_lo, 2)
                    sp.wait_ge(outT_out[1], 16 * NB)
                if j == 2:
                    source(2, h1T_dram, e)
                    if is_static(e) and e == NB - 1:
                        for c in range(RAW):
                            early(c)
                if j in (3, 5, 9, 11):
                    k = (3, 5, 9, 11).index(j)
                    n = TPB * e + k
                    if not is_static(e) or n >= 2:
                        sp.wait_ge(y_ready, n - 1)
                    load(xn[:, k % 2, :], x_rows, n).then_inc(rows_in[k % 2], 16)
                    if is_static(e) and e == NB - 1 and k >= 2:
                        early(RAW + k - 2)
                if is_static(e) and e == NB - 1 and j == 12:
                    early(RAW + 2)

            walk(sp, stream, epilogue1, epilogue2)

        @block.gpsimd
        def _(pool):
            nc.gpsimd.memset(ident[:, :], 0.0).then_inc(ident_zeroed, 1)
            nc.gpsimd.memset(keep["neg_half"][:, :], -0.5).then_inc(constants, 1)
            pool.wait_ge(ident_zeroed, 1)
            nc.gpsimd.affine_select(out=ident[:, :], in_=ident[:, :], compare_op=ALU.not_equal, fill=1.0, base=0,
                                    pattern=[[-1, P]], channel_multiplier=1).then_inc(constants, 1)
            pool.wait_ge(constants, 2)
            with pool.Fori(0, NB) as e:
                for k in range(TPB):
                    n = TPB * e + k
                    pool.wait_ge(veps_ready, n + 1)
                    nc.gpsimd.tensor_tensor(rstd[:, k % 2, :], veps[:, k % 2, :], keep["neg_half"][:, :],
                                            ALU.pow).then_inc(rstd_ready, 1)

        @block.scalar
        def _(act):
            def store(dram, n, value):
                return act.dma_start(dram[ds(n, 1), :, :].rearrange("o p n -> (o p) n"), value)

            def copy(out, value):
                return nc.scalar.activation(out, value, ACT.Copy)

            def stream(layer, b, j):
                g = STEPS * whole(layer, b) + j
                start = layer == 1 and is_static(b) and b == 0
                if start and j % 2 == 0:
                    i = j // 2
                    act.wait_ge(x_in[i % 2], 16 * (i // 2 + 1))
                    copy(X[:, i * XS:(i + 1) * XS, HI, :], x_raw[i % 2]).then_inc(x_hi, 1)
                act.wait_ge(raw_in[j % RAW], 16 * (STEPS // RAW * whole(layer, b) + j // RAW + 1))
                for t in range(2):
                    if not (layer == 1 and is_static(b) and g < 2):
                        act.wait_ge(adj_used, 2 * g + t - 3)
                    copy(adj[:, 2 * (j % 2) + t, HI, :], raw[:, j % RAW, t * ROWS:(t + 1) * ROWS])\
                        .then_inc(adj_hi, 1)
                if start and j == 12:
                    act.wait_ge(w_in, 16)
                    copy(W[:, :, HI, :], w1_raw).then_inc(w_hi, 1)
                if start and j == 14:
                    act.wait_ge(wa_in, 16)
                    copy(WA[:, :, HI, :], wa_raw).then_inc(wa_hi, 1)
                if start and j == 7:
                    act.wait_ge(m_done, 1)
                    copy(M[:, :, HI, :], mP).then_inc(m_hi, 1)

            def sums(layer, e):
                for f in range(FT):
                    if f == 0:
                        act.wait_ge(agg0_done, whole(layer, e) + 1)
                    else:
                        act.wait_ge(adj_used, 2 * STEPS * (whole(layer, e) + 1))
                    if later(e):
                        act.wait_ge(proj_done[layer], (2 if layer == 1 else TPB) * e)
                    elif layer == 2:
                        act.wait_ge(proj_done[1], 2 * NB)
                    copy(agg[:, f, HI, :], aggP[f][:, :]).then_inc(agg_hi, 1)

            def epilogue1(e, j):
                if j == 0:
                    sums(1, e)
                if j == 3:
                    act.wait_ge(src_in[1], 16 * (e + 1))
                    if later(e):
                        act.wait_ge(proj_done[1], 2 * e)
                    copy(src[:, :, HI, :], src_raw[:, :, :]).then_inc(src_hi[1], 1)
                if j in (8, 9):
                    f = j - 8
                    act.wait_ge(proj_done[1], 2 * e + f + 1)
                    if later(e):
                        act.wait_ge(turn_done[1], 2 * e)
                        act.wait_ge(outT_out[1], 16 * e)
                    else:
                        act.wait_ge(x_lo, NX)
                    nc.scalar.activation(outT[:, f, :], projP[f][:, :], ACT.Relu).then_inc(outT_ready[1], 1)
                if j == 10:
                    act.wait_ge(outT_ready[1], 2 * e + 2)
                    store(h1T_dram, e, outT[:, :, :].rearrange("p f n -> p (f n)")).then_inc(outT_out[1], 16)
                if is_static(e) and e == NB - 1 and j == 11:
                    act.wait_ge(w_in, 32)
                    act.wait_ge(proj_done[1], 2 * NB)
                    copy(W[:, :, HI, :], w2_raw).then_inc(w_hi, 1)
                if j == 12:
                    for r in range(2):
                        act.wait_ge(turn_done[1], 2 * e + r + 1)
                        copy(H[:, ds(TPB * e + 2 * r, 2), HI, :],
                             turnP[r][:, :].rearrange("p (t n) -> p t n", t=2)).then_inc(made_hi[1], 1)

            def epilogue2(e, j):
                if j == 2 and later(e):
                    w = e - 1
                    for r in range(2):
                        act.wait_ge(att_done, 2 * w + r + 1)
                        copy(X[:, ds(TPB * w + 2 * r, 2), HI, :],
                             projP[r][:, :].rearrange("p (t n) -> p t n", t=2)).then_inc(made_hi[2], 1)
                if is_static(e) and e == NB:
                    return
                if j == 0:
                    sums(2, e)
                if j == 3:
                    act.wait_ge(src_in[2], 16 * (e + 1))
                    if later(e):
                        act.wait_ge(att_done, 2 * e)
                    copy(src[:, :, HI, :], src_raw[:, :, :]).then_inc(src_hi[2], 1)
                if j in (7, 9, 11, 13):
                    k = (j - 7) // 2
                    n = TPB * e + k
                    act.wait_ge(x1_ready, n + 1)
                    store(x1_dram, n, x1[:, k % 2, :]).then_inc(x1_out[k % 2], 16)
                if j == 13:
                    act.wait_ge(turn_done[2], TPB * e + TPB)
                    act.wait_ge(proj_done[2], TPB * e + TPB)
                    for f in range(FT):
                        copy(src[:, f, HI, :], turnP[f][:, :]).then_inc(x1T_hi, 1)
                if j in (14, 15):
                    f = j - 14
                    act.wait_ge(x1T_lo, 2 * e + f + 1)
                    if later(e):
                        act.wait_ge(outT_out[2], 16 * e)
                    else:
                        act.wait_ge(outT_out[1], 16 * NB)
                    copy(outT[:, f, :], turnP[f][:, :]).then_inc(outT_ready[2], 1)
                if j == 15:
                    act.wait_ge(outT_ready[2], 2 * e + 2)
                    store(x1T_dram, e, outT[:, :, :].rearrange("p f n -> p (f n)")).then_inc(outT_out[2], 16)
                if is_static(e) and e == NB - 1 and j in EARLY_AT:
                    c = EARLY_AT.index(j)
                    act.wait_ge(adj_used, 4 * STEPS * NB)
                    act.wait_ge(xt_in[c % RAW], 16 * (c // RAW + 1))
                    copy(XT[:, :, HI, c * CH:(c + 1) * CH], raw[:, c % RAW, :].rearrange("p (f n) -> p f n", f=FT))\
                        .then_inc(xt_hi, 1)

            walk(act, stream, epilogue1, epilogue2)
            act.wait_ge(outT_out[2], 16 * NB)
            for s in range(2):
                act.wait_ge(x1_out[s], 16 * NT // 2)

        @block.vector
        def _(dve):
            def low(out, value, high):
                return nc.vector.tensor_tensor(out, value, high.bitcast(F32), ALU.subtract)

            def stream(layer, b, j):
                g = STEPS * whole(layer, b) + j
                start = layer == 1 and is_static(b) and b == 0
                if start and j % 2 == 0:
                    i = j // 2
                    at = slice(i * XS, (i + 1) * XS)
                    dve.wait_ge(x_hi, i + 1)
                    low(X[:, at, LO, :], x_raw[i % 2], X[:, at, HI, :]).then_inc(x_lo, 1)
                for t in range(2):
                    at = 2 * (j % 2) + t
                    dve.wait_ge(adj_hi, 2 * g + t + 1)
                    low(adj[:, at, LO, :], raw[:, j % RAW, t * ROWS:(t + 1) * ROWS], adj[:, at, HI, :])\
                        .then_inc(adj_lo, 1)
                if start and j == 12:
                    dve.wait_ge(w_hi, 1)
                    low(W[:, :, LO, :], w1_raw, W[:, :, HI, :]).then_inc(w_lo, 1)
                if start and j == 3:
                    dve.wait_ge(z_done, 1)
                    nc.vector.tensor_copy(z, zP).then_inc(z_ready, 1)
                if start and j == 14:
                    dve.wait_ge(wa_hi, 1)
                    low(WA[:, :, LO, :], wa_raw, WA[:, :, HI, :]).then_inc(wa_lo, 1)
                if start and j == 7:
                    dve.wait_ge(m_hi, 1)
                    low(M[:, :, LO, :], mP, M[:, :, HI, :]).then_inc(m_lo, 1)

            def sums(layer, e):
                for f in range(FT):
                    dve.wait_ge(agg_hi, 2 * whole(layer, e) + f + 1)
                    low(agg[:, f, LO, :], aggP[f][:, :], agg[:, f, HI, :]).then_inc(agg_lo, 1)

            def source(layer, e):
                dve.wait_ge(src_hi[layer], e + 1)
                low(src[:, :, LO, :], src_raw[:, :, :], src[:, :, HI, :]).then_inc(src_lo[layer], 1)

            def made_low(layer, made, banks, w):
                for r in range(2):
                    at = ds(TPB * w + 2 * r, 2)
                    dve.wait_ge(made_hi[layer], 2 * w + r + 1)
                    low(made[:, at, LO, :], banks[r][:, :].rearrange("p (t n) -> p t n", t=2), made[:, at, HI, :])\
                        .then_inc(made_lo[layer], 1)

            def epilogue1(e, j):
                if j == 0:
                    sums(1, e)
                if j == 3:
                    source(1, e)
                if is_static(e) and e == NB - 1 and j == 11:
                    dve.wait_ge(w_hi, 2)
                    low(W[:, :, LO, :], w2_raw, W[:, :, HI, :]).then_inc(w_lo, 1)
                if j == 12:
                    made_low(1, H, turnP, e)

            def epilogue2(e, j):
                if j == 2 and later(e):
                    made_low(2, X, projP, e - 1)
                if is_static(e) and e == NB:
                    return
                if j == 0:
                    sums(2, e)
                if j == 3:
                    source(2, e)
                if j in (5, 7, 9, 11):
                    k = (j - 5) // 2
                    n, s = TPB * e + k, k % 2
                    dve.wait_ge(proj_done[2], n + 1)
                    dve.wait_ge(rows_in[s], 16 * (TPB // 2 * e + k // 2 + 1))
                    nc.vector.scalar_tensor_tensor(out=y[:, s, :], in0=projP[s][:, 0:D], scalar=0.0,
                                                   in1=xn[:, s, :], op0=ALU.max, op1=ALU.add).then_inc(y_ready, 1)
                    dve.wait_ge(y_ready, n + 1)
                    nc.vector.bn_stats(stats[:, s, :], y[:, s, :]).then_inc(stats_ready, 1)
                    dve.wait_ge(stats_ready, n + 1)
                    nc.vector.memset(tick[:, :], 0.0)
                    nc.vector.bn_aggr(mv[:, s, :], stats[:, s, :]).then_inc(mv_ready, 1)
                    dve.wait_ge(mv_ready, n + 1)
                    nc.vector.tensor_scalar_add(veps[:, s, :], mv[:, s, 1:2], EPS).then_inc(veps_ready, 1)
                if j in ((8, 10, 12, 13) if is_static(e) and e == NB - 1 else (6, 8, 10, 12)):
                    k = (8, 10, 12, 13).index(j) if is_static(e) and e == NB - 1 else (j - 6) // 2
                    n, s = TPB * e + k, k % 2
                    dve.wait_ge(rstd_ready, n + 1)
                    if not is_static(e) or n >= 2:
                        dve.wait_ge(x1_out[s], 16 * (TPB // 2 * e + k // 2))
                        dve.wait_ge(turn_done[2], n - 1)
                    elif n == 0:
                        dve.wait_ge(wa_lo, 1)
                    nc.vector.tensor_scalar(x1[:, s, :], y[:, s, :], mv[:, s, 0:1], rstd[:, s, :],
                                            ALU.subtract, ALU.mult).then_inc(x1_ready, 1)
                if j in (13, 14):
                    f = j - 13
                    dve.wait_ge(x1T_hi, 2 * e + f + 1)
                    low(src[:, f, LO, :], turnP[f][:, :], src[:, f, HI, :]).then_inc(x1T_lo, 1)
                if is_static(e) and e == NB - 1 and j in EARLY_AT:
                    c = EARLY_AT.index(j)
                    at = slice(c * CH, (c + 1) * CH)
                    dve.wait_ge(xt_hi, c + 1)
                    low(XT[:, :, LO, at], raw[:, c % RAW, :].rearrange("p (f n) -> p f n", f=FT), XT[:, :, HI, at])\
                        .then_inc(xt_lo, 1)

            walk(dve, stream, epilogue1, epilogue2)

        @block.tensor
        def _(pe):
            def three(out, stat, mov, start, stop):
                nc.tensor.matmul(out, stat(HI), mov(HI), start=start, stop=False)
                nc.tensor.matmul(out, stat(HI), mov(LO), start=False, stop=False)
                return nc.tensor.matmul(out, stat(LO), mov(HI), start=False, stop=stop)

            def small(out, stat, mov):
                for o in range(FT):
                    for k in range(FT):
                        last = nc.tensor.matmul(out[:, o, :], stat[:, k, o * P:(o + 1) * P], mov[:, k, :],
                                                start=k == 0, stop=k == FT - 1)
                return last

            def stream(layer, b, j):
                g = STEPS * whole(layer, b) + j
                node = X if layer == 1 else H
                start = layer == 1 and is_static(b) and b == 0
                if start and j % 2 == 0:
                    pe.wait_ge(x_lo, j // 2 + 1)
                if layer == 2 and is_static(b) and b == 0:
                    if j == 0:
                        pe.wait_ge(made_lo[1], 2 * NB - 2)
                    if j == STEPS - 2:
                        pe.wait_ge(made_lo[1], 2 * NB)
                order = [(t, f) for t in range(2) for f in range(FT)]
                if j in (0, STEPS - 1):
                    order = [(t, f) for f in range(FT) for t in range(2)]
                for t, f in order:
                    if f == 0:
                        pe.wait_ge(adj_lo, 2 * g + t + 1)
                    if j == 0 and t == 0 and not start:
                        pe.wait_ge(agg_lo, 2 * whole(layer, b) + f - 1)
                    last = three(aggP[f][:, :],
                                 lambda h: node[:, 2 * j + t, h, f * P:(f + 1) * P],
                                 lambda h: adj[:, 2 * (j % 2) + t, h, :],
                                 j == 0 and t == 0, j == STEPS - 1 and t == 1)
                    if f == 1:
                        last.then_inc(adj_used, 1)
                    elif j == STEPS - 1 and t == 1:
                        last.then_inc(agg0_done, 1)
                if start and j == 2:
                    pe.wait_ge(t_in, 32)
                    small(zP, uT_raw, waT_raw).then_inc(z_done, 1)
                if start and j == 5:
                    pe.wait_ge(z_ready, 1)
                    small(mP, waT_raw, z).then_inc(m_done, 1)

            def epilogue1(e, j):
                if j in (5, 6):
                    o = j - 5
                    pe.wait_ge(agg_lo, 2 * e + 2)
                    pe.wait_ge(src_lo[1], e + 1)
                    if later(e):
                        pe.wait_ge(outT_ready[1], 2 * e - 1 + o)
                    else:
                        pe.wait_ge(w_lo, 1)
                        pe.wait_ge(m_lo, 1)
                    for kt in range(2 * FT):
                        part = src if kt < FT else agg
                        last = three(projP[o][:, :], lambda h: W[:, kt, h, o * P:(o + 1) * P],
                                     lambda h: part[:, kt % FT, h, :], kt == 0, kt == 2 * FT - 1)
                    last.then_inc(proj_done[1], 1)
                if j == 10:
                    if not later(e):
                        pe.wait_ge(constants, 2)
                    for r in range(2):
                        pe.wait_ge(outT_ready[1], 2 * e + 2)
                        if later(e):
                            pe.wait_ge(made_lo[1], 2 * e - 1 + r)
                        for q in range(2):
                            for f in range(FT):
                                i = 2 * r + q
                                last = nc.tensor.transpose(turnP[r][:, q * D + f * P:q * D + (f + 1) * P],
                                                           outT[:, f, i * P:(i + 1) * P], ident[:, :])
                        last.then_inc(turn_done[1], 1)

            def epilogue2(e, j):
                if is_static(e) and e == NB:
                    return
                if j in (3, 5, 7, 9):
                    k = (j - 3) // 2
                    n = TPB * e + k
                    if k == 0:
                        pe.wait_ge(agg_lo, 2 * whole(2, e) + 2)
                        pe.wait_ge(src_lo[2], e + 1)
                        if not later(e):
                            pe.wait_ge(w_lo, 2)
                    if k >= 2:
                        pe.wait_ge(y_ready, n - 1)
                    elif later(e):
                        pe.wait_ge(made_lo[2], 2 * e - 1 + k)
                    for kt in range(2 * FT):
                        part = src if kt < FT else agg
                        last = three(projP[k % 2][:, 0:D], lambda h: part[:, kt % FT, h, k * P:(k + 1) * P],
                                     lambda h: W[:, kt, h, :], kt == 0, kt == 2 * FT - 1)
                    last.then_inc(proj_done[2], 1)
                if j in (6, 8, 10, 12):
                    k = (j - 6) // 2
                    n = TPB * e + k
                    pe.wait_ge(x1_ready, n + 1)
                    if k == 0 and later(e):
                        pe.wait_ge(outT_ready[2], 2 * e)
                    for f in range(FT):
                        last = nc.tensor.transpose(turnP[f][:, k * P:(k + 1) * P],
                                                   x1[:, k % 2, f * P:(f + 1) * P], ident[:, :])
                    last.then_inc(turn_done[2], 1)
                if j == 15:
                    pe.wait_ge(x1T_lo, 2 * e + 2)
                    pe.wait_ge(y_ready, TPB * e + TPB)
                    if not later(e):
                        pe.wait_ge(wa_lo, 1)
                    for r in range(2):
                        for q in range(2):
                            i = 2 * r + q
                            for f in range(FT):
                                last = three(projP[r][:, q * D:(q + 1) * D],
                                             lambda h: src[:, f, h, i * P:(i + 1) * P],
                                             lambda h: WA[:, f, h, :], f == 0, f == FT - 1)
                        last.then_inc(att_done, 1)

            walk(pe, stream, epilogue1, epilogue2)


def attention(nc, keep, adj_dram, x1T_dram, x1_dram, out):
    H, XT, M, ident = keep["X"], x1T_view(keep), keep["M"], keep["ident"]
    SLOTS = 16
    BODY = 16
    LAST = NT * NC

    with ExitStack() as ctx:
        def sb(name, shape, dt):
            return ctx.enter_context(nc.sbuf_tensor(name, shape, dt))

        def ps(name, shape=(P, 512)):
            return ctx.enter_context(nc.psum_tensor(name, list(shape), F32))

        def sem(name):
            return ctx.enter_context(nc.semaphore(name))

        adj = sb("adj", [P, SLOTS, CH], F32)
        pm = sb("pm", [P, NC + 1, CH], F32)
        bias = sb("bias", [P, 2, CH], BF16)
        turned = sb("turned", [P, 2, 2, CH], F32R)
        strip = sb("strip", [P, (2 * NC - 1) * P], BF16)
        q = sb("q", [P, FT, 2, 2 * P], F32R)
        mx, sums = sb("mx", [P, 2, NC], F32), sb("sums", [P, 2, NC], F32)
        mrow, nmax = sb("mrow", [P, 2, 1], F32), sb("nmax", [P, 2, 1], F32)
        rsum, rinv = sb("rsum", [P, 2, 1], F32), sb("rinv", [P, 2, 1], F32)
        tick = sb("tick_att", [P, 1], F32)
        cross = sb("cross", [P, D], F32)
        both = sb("both", [P, D], F32)
        x1 = sb("x1_rows", [P, 2, D], F32)
        y = sb("y_att", [P, D], F32)
        fin = sb("fin", [P, 2, D], F32)
        stats, mv = sb("stats_att", [P, 2, 6], F32), sb("mv_att", [P, 2, 2], F32)
        veps, rstd = sb("veps_att", [P, 2, 1], F32), sb("rstd_att", [P, 2, 1], F32)
        scoreP = [ps(f"scoreP{i}") for i in range(4)]
        turnP = [ps("turn_att0"), ps("turn_att1")]
        accP = ps("accP")
        qP = ps("qP", (P, FT, 2 * P))

        adj_in = [sem(f"adj_in{i}") for i in range(SLOTS // 2)]
        xt_in = [sem(f"xt_in{i}") for i in range(NC - EARLY)]
        x1_in = [sem("x1_in0"), sem("x1_in1")]
        out_sent = [sem("out_sent0"), sem("out_sent1")]
        xt_hi, xt_lo = sem("xt_hi"), sem("xt_lo")
        zeroed, strip_ready = sem("zeroed_strip"), sem("strip_ready")
        q_done, q_hi, q_lo = sem("q_done"), sem("q_hi"), sem("q_lo")
        diag_added, bias_ready = sem("diag_added"), sem("bias_ready")
        scores_done, masked, mrow_ready, nmax_ready = (sem(n) for n in
                                                       ("scores_done", "masked", "mrow_ready", "nmax_ready"))
        exp_done, weighted, turn_done = sem("exp_done"), sem("weighted"), sem("turn_att_done")
        turned_hi, turned_lo, av_done = sem("turned_hi"), sem("turned_lo"), sem("av_done")
        cross_ready, acc_read, rsum_ready, rinv_ready = (sem(n) for n in
                                                         ("cross_ready", "acc_read", "rsum_ready", "rinv_ready"))
        y_ready, stats_ready, mv_ready = sem("y_att_ready"), sem("stats_att_ready"), sem("mv_att_ready")
        veps_ready, rstd_ready, fin_ready = sem("veps_att_ready"), sem("rstd_att_ready"), sem("fin_ready")

        def slot(a):
            return NC if a == 2 * NC - 1 else a % NC

        def walk(eng, step, tail=BODY + 2):
            for s in range(BODY):
                step(0, s)
            with eng.Fori(1, NT // 2 - 1) as k:
                for s in range(BODY):
                    step(k, s)
            for s in range(BODY + tail):
                step(NT // 2 - 1 + s // BODY, s % BODY)

        def live(k, s, back):
            return not is_static(k) or 0 <= BODY * k + s - back < LAST

        block = ctx.enter_context(nc.Block())

        @block.sync
        def _(sp):
            def adj_load(k, s8):
                w = SLOTS // 2 * k + s8
                sp.dma_start(adj[:, 2 * s8:2 * s8 + 2, :].rearrange("p c n -> p (c n)"),
                             adj_dram[ds(w, 1), :, :].rearrange("o p n -> (o p) n")).then_inc(adj_in[s8], 16)

            def x1_load(n, s):
                sp.dma_start(x1[:, s, :], x1_dram[ds(n, 1), :, :].rearrange("o p n -> (o p) n"))\
                    .then_inc(x1_in[s], 16)

            for s8 in range(4):
                adj_load(0, s8)
                if s8 < NC - EARLY:
                    sp.dma_start(adj[:, 8 + 2 * s8:10 + 2 * s8, :], x1T_dram[EARLY + s8, :, :]
                                 .rearrange("p (f n) -> p f n", f=FT)).then_inc(xt_in[s8], 16)
            for n in range(2):
                x1_load(n, n)
            for s8 in range(4, 8):
                if s8 - 4 < NC - EARLY:
                    sp.wait_ge(xt_lo, s8 - 3)
                adj_load(0, s8)

            def store(n, s):
                sp.wait_ge(fin_ready, n + 1)
                sp.dma_start(out[ds(n, 1), :, :].rearrange("o p n -> (o p) n"), fin[:, s, :])\
                    .then_inc(out_sent[s], 16)

            def turnover(n, u):
                store(n, u)
                sp.wait_ge(y_ready, n + 1)
                x1_load(n + 2, u)

            def pair(k):
                for s8 in range(8):
                    sp.wait_ge(weighted, 16 * k + 2 * s8 - 14)
                    adj_load(k, s8)
                    if s8 == 3 and (not is_static(k) or k >= 2):
                        turnover(2 * k - 3, 1)
                    if s8 == 7:
                        turnover(2 * k - 2, 0)

            pair(1)
            with sp.Fori(2, NT // 2) as k:
                pair(k)
            turnover(NT - 3, 1)
            store(NT - 2, 0)
            store(NT - 1, 1)
            for s in range(2):
                sp.wait_ge(out_sent[s], 16 * NT // 2)

        @block.gpsimd
        def _(pool):
            def diag(k, s, ahead):
                p, s = k + (s + ahead) // BODY, (s + ahead) % BODY
                u, c = s // NC, s % NC
                pool.wait_ge(adj_in[s // 2], 16 * (p + 1))
                col = s * CH + (p % 2) * (2 * P) + u * P
                off = (NC - 1 - c) * P + (p // 2) * P
                at = adj[:, :, :].rearrange("p c n -> p (c n)")[:, ds(col, P)]
                nc.gpsimd.tensor_tensor(at, at, strip[:, ds(off, P)], ALU.add).then_inc(diag_added, 1)

            def step(k, s):
                if live(k, s, 8):
                    t = BODY * k + s - 8
                    a = (s - 8) % BODY
                    pool.wait_ge(exp_done, t + 1)
                    nc.gpsimd.tensor_tensor(pm[:, slot(a), :], pm[:, slot(a), :], adj[:, a, :], ALU.mult)\
                        .then_inc(weighted, 1)
                if live(k, s, -4):
                    diag(k, s, 4)
                if s % NC == 4 and (not is_static(k) or 0 <= 2 * k + s // NC - 2 < NT):
                    n = 2 * k + s // NC - 2
                    r = s // NC
                    pool.wait_ge(veps_ready, n + 1)
                    nc.gpsimd.tensor_tensor(rstd[:, r, :], veps[:, r, :], keep["neg_half"][:, :], ALU.pow)\
                        .then_inc(rstd_ready, 1)

            nc.gpsimd.memset(strip[:, :], 0.0).then_inc(zeroed, 1)
            pool.wait_ge(zeroed, 1)
            mid = strip[:, (NC - 1) * P:NC * P]
            nc.gpsimd.affine_select(out=mid, in_=mid, compare_op=ALU.not_equal, fill=1.0, base=0,
                                    pattern=[[-1, P]], channel_multiplier=1).then_inc(strip_ready, 1)
            pool.wait_ge(strip_ready, 1)
            for s in range(4):
                diag(0, s, 0)
            walk(pool, step)

        @block.scalar
        def _(act):
            def xt_high(i):
                act.wait_ge(xt_in[i], 16)
                nc.scalar.activation(XT[:, :, HI, (EARLY + i) * CH:(EARLY + i + 1) * CH],
                                     adj[:, 8 + 2 * i:10 + 2 * i, :], ACT.Copy).then_inc(xt_hi, 1)

            def q_high(pair, u):
                act.wait_ge(q_done, pair + 1)
                at = slice(u * P, (u + 1) * P)
                nc.scalar.activation(q[:, :, HI, at], qP[:, :, at], ACT.Copy).then_inc(q_hi, 1)

            def step(k, s):
                if is_static(k) and k == 0 and s < NC - EARLY:
                    xt_high(s)
                if s == 12 and (not is_static(k) or k + 1 < NT // 2):
                    act.wait_ge(scores_done, BODY * k + NC)
                    q_high(k + 1, 0)
                if s == 1 and (not is_static(k) or 1 <= k < NT // 2):
                    act.wait_ge(scores_done, BODY * k)
                    q_high(k, 1)
                if live(k, s, 8):
                    t, a = BODY * k + s - 8, (s - 8) % BODY
                    u, c = a // NC, a % NC
                    if c == 0:
                        m = 2 * k + (s - 8) // NC
                        act.wait_ge(nmax_ready, m + 1)
                    nc.scalar.activation(pm[:, slot(a), :], pm[:, slot(a), :], ACT.Exp, bias=nmax[:, u, :],
                                         accum_out=sums[:, u, c:c + 1]).then_inc(exp_done, 1)
                if live(k, s, 9):
                    t, c = BODY * k + s - 9, (s - 9) % NC
                    act.wait_ge(turn_done, t + 1)
                    if not is_static(k) or t >= 2:
                        act.wait_ge(av_done, t - 1)
                    nc.scalar.activation(turned[:, c % 2, HI, :], turnP[c % 2][:, :], ACT.Copy)\
                        .then_inc(turned_hi, 1)
                if s % NC == 1 and (not is_static(k) or 0 <= 2 * k + s // NC - 2 < NT):
                    n = 2 * k + s // NC - 2
                    act.wait_ge(av_done, NC * n + NC)
                    if not is_static(k) or n >= 1:
                        act.wait_ge(acc_read, n)
                    nc.scalar.activation(cross[:, :], accP[:, D:2 * D], ACT.Copy).then_inc(cross_ready, 1)

            q_high(0, 0)
            q_high(0, 1)
            walk(act, step)

        @block.vector
        def _(dve):
            def low(out, value, high):
                return nc.vector.tensor_tensor(out, value, high, ALU.subtract)

            def xt_low(i):
                at = slice((EARLY + i) * CH, (EARLY + i + 1) * CH)
                dve.wait_ge(xt_hi, i + 1)
                low(XT[:, :, LO, at], adj[:, 8 + 2 * i:10 + 2 * i, :], XT[:, :, HI, at].bitcast(F32)).then_inc(xt_lo, 1)

            def q_low(pair, u):
                dve.wait_ge(q_hi, 2 if is_static(pair) and pair == 0 else 2 * pair + u + 1)
                at = slice(u * P, (u + 1) * P)
                low(q[:, :, LO, at], qP[:, :, at], q[:, :, HI, at].bitcast(F32)).then_inc(q_lo, 1)

            def mask_bias(k, s, ahead):
                t, a = BODY * k + s + ahead, (s + ahead) % BODY
                if not is_static(k) or t >= 2:
                    dve.wait_ge(masked, t - 1)
                dve.wait_ge(diag_added, t + 1)
                nc.vector.tensor_scalar(bias[:, a % 2, :], adj[:, a, :], 0.0, -BIG, ALU.is_le, ALU.mult)\
                    .then_inc(bias_ready, 1)

            def step(k, s):
                if is_static(k) and k == 0 and s < NC - EARLY:
                    xt_low(s)
                if live(k, s, 9):
                    t, c = BODY * k + s - 9, (s - 9) % NC
                    dve.wait_ge(turned_hi, t + 1)
                    low(turned[:, c % 2, LO, :], turnP[c % 2][:, :], turned[:, c % 2, HI, :].bitcast(F32))\
                        .then_inc(turned_lo, 1)
                if s % NC == 1 and (not is_static(k) or 0 <= 2 * k + s // NC - 2 < NT):
                    n = 2 * k + s // NC - 2
                    dve.wait_ge(cross_ready, n + 1)
                    if not is_static(k) or n >= 1:
                        dve.wait_ge(y_ready, n)
                    nc.vector.tensor_tensor(both[:, :], accP[:, 0:D], cross[:, :], ALU.add).then_inc(acc_read, 1)
                if live(k, s, 0):
                    t, u, c = BODY * k + s, s // NC, s % NC
                    dve.wait_ge(scores_done, t + 1)
                    dve.wait_ge(bias_ready, t + 1)
                    back = 2 * NC if c == NC - 1 else NC
                    if not is_static(k) or t >= back:
                        dve.wait_ge(turn_done, t - back + 1)
                    if not is_static(k) or t >= 1:
                        dve.wait_ge(masked, t)
                    nc.vector.memset(tick[:, :], 0.0)
                    nc.vector.tensor_tensor_reduce(out=pm[:, slot(s), :], in0=scoreP[s % 4][:, :], in1=bias[:, s % 2, :],
                                                   scale=1.0, scalar=-2.0 * BIG, op0=ALU.add, op1=ALU.max,
                                                   accum_out=mx[:, u, c:c + 1]).then_inc(masked, 1)
                    if c == NC - 1:
                        m = 2 * k + u
                        dve.wait_ge(masked, t + 1)
                        nc.vector.reduce_max(mrow[:, u, :], mx[:, u, :], AX.X).then_inc(mrow_ready, 1)
                        dve.wait_ge(mrow_ready, m + 1)
                        nc.vector.tensor_scalar_mul(nmax[:, u, :], mrow[:, u, :], -1.0).then_inc(nmax_ready, 1)
                if live(k, s, -1):
                    mask_bias(k, s, 1)
                if s == 12 and (not is_static(k) or k + 1 < NT // 2):
                    q_low(k + 1, 0)
                if s == 1 and (not is_static(k) or 1 <= k < NT // 2):
                    q_low(k, 1)
                if s % NC == 2 and (not is_static(k) or 0 <= 2 * k + s // NC - 2 < NT):
                    n, r = 2 * k + s // NC - 2, s // NC
                    nc.vector.reduce_sum(rsum[:, r, :], sums[:, r, :], AX.X).then_inc(rsum_ready, 1)
                    dve.wait_ge(rsum_ready, n + 1)
                    nc.vector.reciprocal(rinv[:, r, :], rsum[:, r, :]).then_inc(rinv_ready, 1)
                    dve.wait_ge(rinv_ready, n + 1)
                    dve.wait_ge(acc_read, n + 1)
                    dve.wait_ge(x1_in[r], 16 * k)
                    nc.vector.scalar_tensor_tensor(out=y[:, :], in0=both[:, :], scalar=rinv[:, r, :],
                                                   in1=x1[:, r, :], op0=ALU.mult, op1=ALU.add).then_inc(y_ready, 1)
                if s % NC == 3 and (not is_static(k) or 0 <= 2 * k + s // NC - 2 < NT):
                    n, r = 2 * k + s // NC - 2, s // NC
                    dve.wait_ge(y_ready, n + 1)
                    nc.vector.bn_stats(stats[:, r, :], y[:, :]).then_inc(stats_ready, 1)
                    dve.wait_ge(stats_ready, n + 1)
                    nc.vector.memset(tick[:, :], 0.0)
                    nc.vector.bn_aggr(mv[:, r, :], stats[:, r, :]).then_inc(mv_ready, 1)
                    dve.wait_ge(mv_ready, n + 1)
                    nc.vector.tensor_scalar_add(veps[:, r, :], mv[:, r, 1:2], EPS).then_inc(veps_ready, 1)
                if s % NC == 6 and (not is_static(k) or 0 <= 2 * k + s // NC - 2 < NT):
                    n, r = 2 * k + s // NC - 2, s // NC
                    dve.wait_ge(rstd_ready, n + 1)
                    if not is_static(k) or n >= 2:
                        dve.wait_ge(out_sent[r], 16 * (k - 1))
                    nc.vector.tensor_scalar(fin[:, r, :], y[:, :], mv[:, r, 0:1], rstd[:, r, :],
                                            ALU.subtract, ALU.mult).then_inc(fin_ready, 1)

            q_low(0, 0)
            q_low(0, 1)
            mask_bias(0, 0, 0)
            walk(dve, step)

        @block.tensor
        def _(pe):
            def three(out, stat, mov, start, stop):
                nc.tensor.matmul(out, stat(HI), mov(HI), start=start, stop=False)
                nc.tensor.matmul(out, stat(HI), mov(LO), start=False, stop=False)
                return nc.tensor.matmul(out, stat(LO), mov(HI), start=False, stop=stop)

            def q_pair(pair):
                for o in range(FT):
                    for f in range(FT):
                        last = three(qP[:, o, :], lambda h: M[:, f, h, o * P:(o + 1) * P],
                                     lambda h: XT[:, f, h, ds(2 * P * pair, 2 * P)], f == 0, f == FT - 1)
                last.then_inc(q_done, 1)

            def step(k, s):
                if live(k, s, 0):
                    t, u, c = BODY * k + s, s // NC, s % NC
                    if s == 0 or s == NC:
                        pe.wait_ge(q_lo, 2 * k + u + 1)
                    if is_static(k) and k == 0 and EARLY <= s < NC:
                        pe.wait_ge(xt_lo, s - EARLY + 1)
                    if not is_static(k) or t >= 4:
                        pe.wait_ge(masked, t - 3)
                    for f in range(FT):
                        last = three(scoreP[s % 4][:, :], lambda h: q[:, f, h, u * P:(u + 1) * P],
                                     lambda h: XT[:, f, h, c * CH:(c + 1) * CH], f == 0, f == FT - 1)
                    last.then_inc(scores_done, 1)
                if s == 10 and (not is_static(k) or k + 1 < NT // 2):
                    pe.wait_ge(q_lo, 2 * k + 2)
                    q_pair(k + 1)
                if live(k, s, 9):
                    t, a = BODY * k + s - 9, (s - 9) % BODY
                    c = a % NC
                    pe.wait_ge(weighted, t + 1)
                    if not is_static(k) or t >= 2:
                        pe.wait_ge(turned_lo, t - 1)
                    for i in range(CH // P):
                        last = nc.tensor.transpose(turnP[c % 2][:, i * P:(i + 1) * P],
                                                   pm[:, slot(a), i * P:(i + 1) * P], ident[:, :])
                    last.then_inc(turn_done, 1)
                if live(k, s, 10):
                    t, c = BODY * k + s - 10, (s - 10) % NC
                    pe.wait_ge(turned_lo, t + 1)
                    if c == 0:
                        m = 2 * k + (s - 10) // NC
                        if not is_static(k) or m >= 1:
                            pe.wait_ge(acc_read, m)
                    for i in range(CH // P):
                        j = c * (CH // P) + i
                        at = slice(i * P, (i + 1) * P)
                        nc.tensor.matmul(accP[:, :], turned[:, c % 2, HI, at],
                                         H[:, j, :, :].rearrange("p h n -> p (h n)"),
                                         start=j == 0, stop=False)
                        last = nc.tensor.matmul(accP[:, 0:D], turned[:, c % 2, LO, at], H[:, j, HI, :],
                                                start=False, stop=j == NT - 1)
                    last.then_inc(av_done, 1)

            q_pair(0)
            walk(pe, step)


def build(nc, x_nodes, x_rows, xT, adjT, adjN, w1, w2, wa, waT, uT, out):
    h1T = nc.dram_tensor("h1T", (NB, P, FT * ROWS), F32, kind="Internal").ap()
    x1T = nc.dram_tensor("x1T", (NB, P, FT * ROWS), F32, kind="Internal").ap()
    x1 = nc.dram_tensor("x1d", (NT, P, D), F32, kind="Internal").ap()
    with ExitStack() as ctx:
        def sb(where, name, shape, dt):
            return where.enter_context(nc.sbuf_tensor(name, shape, dt))

        keep = {
            "X": sb(ctx, "node_x", [P, NT, 2, D], F32R),
            "H": sb(ctx, "node_h", [P, NT, 2, D], F32R),
            "M": sb(ctx, "score_m", [P, FT, 2, D], F32R),
            "ident": sb(ctx, "ident", [P, P], F32),
            "neg_half": sb(ctx, "neg_half", [P, 1], F32),
        }
        with ExitStack() as first:
            keep["WA"] = sb(first, "wa_parts", [P, FT, 2, D], F32R)
            convolutions(nc, keep, adjT, xT, x_nodes, x_rows, w1, w2, wa, waT, uT, h1T, x1T, x1)
        attention(nc, keep, adjN, x1T, x1, out)


def kernel(x, adj, L0_gnn_W1, L0_gnn_W2, L1_gnn_W, L1_gnn_U):
    import numpy as np
    import concourse.bacc as bacc
    from concourse.bass_utils import run_bass_kernel_spmd

    x, adj = np.asarray(x), np.asarray(adj)
    tiles = lambda w: np.ascontiguousarray(np.asarray(w).reshape(-1, P, D).transpose(1, 0, 2))
    arrays = {
        "x_nodes": tiles(x),
        "x_rows": x.reshape(NT, P, D),
        "xT": np.ascontiguousarray(x.reshape(NB, ROWS, FT, P).transpose(0, 3, 2, 1)).reshape(NB, P, FT * ROWS),
        "adjT": np.ascontiguousarray(adj.reshape(NB, ROWS, STEPS, 2, P).transpose(0, 2, 4, 3, 1))
        .reshape(NB * STEPS, P, 2 * ROWS),
        "adjN": np.ascontiguousarray(adj.reshape(NT, P, NC // 2, 2 * CH).transpose(0, 2, 1, 3))
        .reshape(NT * NC // 2, P, 2 * CH),
        "w1": tiles(L0_gnn_W1),
        "w2": tiles(L0_gnn_W2),
        "wa": tiles(L1_gnn_W),
        "waT": tiles(np.asarray(L1_gnn_W).T),
        "uT": tiles(np.asarray(L1_gnn_U).T),
    }
    nc = bacc.Bacc("TRN2", target_bir_lowering=False, num_devices=1)
    args = [nc.dram_tensor(n, a.shape, mybir.dt.from_np(a.dtype), kind="ExternalInput").ap()
            for n, a in arrays.items()]
    out = nc.dram_tensor("out", (NT, P, D), F32, kind="ExternalOutput").ap()
    build(nc, *args, out)
    r = run_bass_kernel_spmd(nc, [arrays], core_ids=[0])
    return r.results[0]["out"].reshape(N, D)
```

```python
from contextlib import ExitStack

import concourse.bass as bass
from concourse import mybir

F32 = mybir.dt.float32
F32R = mybir.dt.float32r
BF16 = mybir.dt.bfloat16
ALU = mybir.AluOpType
ACT = mybir.ActivationFunctionType
AX = mybir.AxisListType
ds = bass.ds

P = 128
N = 4096
D = 256
FT = D // P
ROWS = 512
NB = N // ROWS
NT = N // P
TPB = ROWS // P
STEPS = 16
RAW = 4
CH = 512
NC = N // CH
EARLY = 7
POOL_EARLY, DVE_EARLY = (0, 4), (1, 2, 3, 5, 6)
HI, LO = 0, 1
EPS = 1e-5
BIG = 1e30


def is_static(v):
    return isinstance(v, int)


def x1T_view(keep):
    return keep["H"].rearrange("p t h n -> p (t h n)").rearrange("p (f h n) -> p f h n", f=FT, h=2)


def convolutions(nc, keep, adjT, xT, x_nodes, x_rows, w1, w2, wa, waT, uT, h1T_dram, x1T_dram, x1_dram):
    X, H, WA, M, ident = (keep[n] for n in ("X", "H", "WA", "M", "ident"))
    XT = x1T_view(keep)
    XS = 4
    NX = NT // XS

    with ExitStack() as ctx:
        def sb(name, shape, dt):
            return ctx.enter_context(nc.sbuf_tensor(name, shape, dt))

        def ps(name):
            return ctx.enter_context(nc.psum_tensor(name, [P, 512], F32))

        def sem(name):
            return ctx.enter_context(nc.semaphore(name))

        raw = sb("adj_raw", [P, RAW, 2 * ROWS], F32)
        adj = sb("adj_parts", [P, 4, 2, ROWS], F32R)
        agg = sb("agg_parts", [P, FT, 2, ROWS], F32R)
        src = sb("src_parts", [P, FT, 2, ROWS], F32R)
        src_raw = sb("src_raw", [P, FT, ROWS], F32)
        outT = sb("outT", [P, FT, ROWS], F32)
        W = sb("w_parts", [P, 2 * FT, 2, D], F32R)
        rows = sb("rows", [P, 3, 2, D], F32)
        xn, y, x1 = (rows[:, i, :, :] for i in range(3))
        stats, mv = sb("stats", [P, 2, 6], F32), sb("mv", [P, 2, 2], F32)
        veps, rstd = sb("veps", [P, 2, 1], F32), sb("rstd", [P, 2, 1], F32)
        tick = sb("tick", [P, 1], F32)
        aggP = [ps("aggP0"), ps("aggP1")]
        projP = [ps("projP0"), ps("projP1")]
        turnP = [ps("turnP0"), ps("turnP1")]
        tail_banks = aggP + projP
        tail_x1 = [x1[:, 0, :], x1[:, 1, :], src_raw[:, 0, 0:D], src_raw[:, 1, 0:D]]

        as_tiles = lambda buf: buf.rearrange("p f n -> p (f n)").rearrange("p (k n) -> p k n", n=D)
        x_raw = [as_tiles(src_raw[:, :, :]), as_tiles(outT[:, :, :])]
        waT_raw, uT_raw, z = xn, y, x1
        w1_raw, wa_raw = rows[:, 0:2, :, :].rearrange("p a k n -> p (a k) n"), x1
        w2_raw = as_tiles(src_raw[:, :, :])
        zP, mP = (projP[i][:, :].rearrange("p (f n) -> p f n", f=FT) for i in range(2))

        raw_in = [sem(f"raw_in{i}") for i in range(RAW)]
        adj_hi, adj_lo, adj_used = sem("adj_hi"), sem("adj_lo"), sem("adj_used")
        agg0_done, agg_hi, agg_lo = sem("agg0_done"), sem("agg_hi"), sem("agg_lo")
        ident_zeroed, constants = sem("ident_zeroed"), sem("constants")
        x_in = [sem("x_in0"), sem("x_in1")]
        x_hi, x_lo = sem("x_hi"), sem("x_lo")
        w_in, w_hi, w_lo = sem("w_in"), sem("w_hi"), sem("w_lo")
        wa_in, wa_hi, wa_lo = sem("wa_in"), sem("wa_hi"), sem("wa_lo")
        t_in, z_done, z_ready = sem("t_in"), sem("z_done"), sem("z_ready")
        m_done, m_hi, m_lo = sem("m_done"), sem("m_hi"), sem("m_lo")
        src_in, src_hi, src_lo, proj_done, turn_done, outT_ready, outT_out, made_hi, made_lo = (
            {layer: sem(f"{name}_l{layer}") for layer in (1, 2)} for name in
            ("src_in", "src_hi", "src_lo", "proj_done", "turn_done", "outT_ready", "outT_out", "made_hi", "made_lo"))
        rows_in = [sem("rows_in0"), sem("rows_in1")]
        x1_out = [sem("x1_out0"), sem("x1_out1")]
        y_ready, stats_ready, mv_ready = sem("y_ready"), sem("stats_ready"), sem("mv_ready")
        veps_ready, rstd_ready, x1_ready = sem("veps_ready"), sem("rstd_ready"), sem("x1_ready")
        x1T_hi, x1T_lo, att_done = sem("x1T_hi"), sem("x1T_lo"), sem("att_done")
        xt_in = [sem(f"xt_early{i}") for i in range(RAW)]
        xt_hi, xt_lo, xt_lo_pool = sem("xt_early_hi"), sem("xt_early_lo"), sem("xt_early_lo_pool")

        def walk(eng, stream, epilogue1, epilogue2, finish):
            for b in range(2):
                for j in range(STEPS):
                    stream(1, b, j)
                    if b >= 1:
                        epilogue1(b - 1, j)
            with eng.Fori(2, NB) as b:
                for j in range(STEPS):
                    stream(1, b, j)
                    epilogue1(b - 1, j)
            for j in range(STEPS):
                stream(2, 0, j)
                epilogue1(NB - 1, j)
            for j in range(STEPS):
                stream(2, 1, j)
                epilogue2(0, j)
            with eng.Fori(2, NB) as b:
                for j in range(STEPS):
                    stream(2, b, j)
                    epilogue2(b - 1, j)
            finish(NB - 1)

        def whole(layer, b):
            return NB * (layer - 1) + b

        def before(layer, b):
            return (1, NB - 1) if layer == 2 and is_static(b) and b == 0 else (layer, b - 1)

        def later(e):
            return not is_static(e) or e >= 1

        block = ctx.enter_context(nc.Block())

        @block.sync
        def _(sp):
            def load(out, dram, n):
                return sp.dma_start(out, dram[ds(n, 1), :, :].rearrange("o p n -> (o p) n"))

            def stream(layer, b, j):
                g = STEPS * whole(layer, b) + j
                start = layer == 1 and is_static(b) and b == 0
                if start and j % 2 == 0:
                    i = j // 2
                    if i >= 2:
                        sp.wait_ge(x_lo, i - 1)
                    sp.dma_start(x_raw[i % 2], x_nodes[:, i * XS:(i + 1) * XS, :]).then_inc(x_in[i % 2], 16)
                if not (layer == 1 and is_static(b) and g < RAW):
                    sp.wait_ge(adj_lo, 2 * (g - RAW + 1))
                load(raw[:, j % RAW, :], adjT, STEPS * b + j).then_inc(raw_in[j % RAW], 16)
                if start and j == 2:
                    sp.dma_start(waT_raw, waT).then_inc(t_in, 16)
                    sp.dma_start(uT_raw, uT).then_inc(t_in, 16)
                if start and j == 9:
                    sp.wait_ge(m_done, 1)
                    sp.dma_start(w1_raw, w1).then_inc(w_in, 16)
                    sp.dma_start(wa_raw, wa).then_inc(wa_in, 16)

            def source(layer, dram, e):
                if later(e):
                    sp.wait_ge(src_lo[layer], e)
                elif layer == 1:
                    sp.wait_ge(x_lo, NX - 1)
                load(src_raw[:, :, :].rearrange("p f n -> p (f n)"), dram, e).then_inc(src_in[layer], 16)

            def epilogue1(e, j):
                if j == 0:
                    source(1, xT, e)
                if is_static(e) and e == NB - 1 and j == 8:
                    sp.wait_ge(src_lo[1], NB)
                    sp.dma_start(w2_raw, w2).then_inc(w_in, 16)

            def x_load(e, k):
                n = TPB * e + k
                if not is_static(n) or n >= 2:
                    sp.wait_ge(y_ready, n - 1)
                load(xn[:, k % 2, :], x_rows, n).then_inc(rows_in[k % 2], 16)

            def early(c):
                sp.wait_ge(outT_out[2], 16 * (c + 1))
                if c < RAW:
                    sp.wait_ge(adj_lo, 4 * STEPS * NB - 2 * (RAW - 1 - c))
                else:
                    if c - RAW in POOL_EARLY:
                        sp.wait_ge(xt_lo_pool, POOL_EARLY.index(c - RAW) + 1)
                    else:
                        sp.wait_ge(xt_lo, DVE_EARLY.index(c - RAW) + 1)
                load(raw[:, c % RAW, :], x1T_dram, c).then_inc(xt_in[c % RAW], 16)

            def epilogue2(e, j):
                if is_static(e) and e == 0 and j == 2:
                    sp.wait_ge(w_lo, 2)
                    sp.wait_ge(outT_out[1], 16 * NB)
                if j == 2:
                    source(2, h1T_dram, e)
                if j in (3, 5, 9, 11):
                    x_load(e, (3, 5, 9, 11).index(j))

            def finish(e):
                source(2, h1T_dram, e)
                for c in range(RAW):
                    early(c)
                for k in range(TPB):
                    x_load(e, k)
                for c in range(RAW, EARLY):
                    early(c)

            walk(sp, stream, epilogue1, epilogue2, finish)

        @block.gpsimd
        def _(pool):
            nc.gpsimd.memset(ident[:, :], 0.0).then_inc(ident_zeroed, 1)
            nc.gpsimd.memset(keep["neg_half"][:, :], -0.5).then_inc(constants, 1)
            pool.wait_ge(ident_zeroed, 1)
            nc.gpsimd.affine_select(out=ident[:, :], in_=ident[:, :], compare_op=ALU.not_equal, fill=1.0, base=0,
                                    pattern=[[-1, P]], channel_multiplier=1).then_inc(constants, 1)
            pool.wait_ge(constants, 2)

            def deviations(e):
                for k in range(TPB):
                    n = TPB * e + k
                    pool.wait_ge(veps_ready, n + 1)
                    nc.gpsimd.tensor_tensor(rstd[:, k % 2, :], veps[:, k % 2, :], keep["neg_half"][:, :],
                                            ALU.pow).then_inc(rstd_ready, 1)

            def early(c):
                at = slice(c * CH, (c + 1) * CH)
                pool.wait_ge(xt_hi, c + 1)
                nc.gpsimd.tensor_tensor(XT[:, :, LO, at], raw[:, c % RAW, :].rearrange("p (f n) -> p f n", f=FT),
                                        XT[:, :, HI, at].bitcast(F32), ALU.subtract).then_inc(xt_lo_pool, 1)

            with pool.Fori(0, NB - 1) as e:
                deviations(e)
            early(POOL_EARLY[0])
            deviations(NB - 1)
            for c in POOL_EARLY[1:]:
                early(c)

        @block.scalar
        def _(act):
            def store(dram, n, value):
                return act.dma_start(dram[ds(n, 1), :, :].rearrange("o p n -> (o p) n"), value)

            def copy(out, value):
                return nc.scalar.activation(out, value, ACT.Copy)

            def stream(layer, b, j):
                g = STEPS * whole(layer, b) + j
                start = layer == 1 and is_static(b) and b == 0
                if start and j % 2 == 0:
                    i = j // 2
                    act.wait_ge(x_in[i % 2], 16 * (i // 2 + 1))
                    copy(X[:, i * XS:(i + 1) * XS, HI, :], x_raw[i % 2]).then_inc(x_hi, 1)
                act.wait_ge(raw_in[j % RAW], 16 * (STEPS // RAW * whole(layer, b) + j // RAW + 1))
                for t in range(2):
                    if not (layer == 1 and is_static(b) and g < 2):
                        act.wait_ge(adj_used, 2 * g + t - 3)
                    copy(adj[:, 2 * (j % 2) + t, HI, :], raw[:, j % RAW, t * ROWS:(t + 1) * ROWS])\
                        .then_inc(adj_hi, 1)
                    if j < FT and t == 0 and not start:
                        sums(*before(layer, b), j)
                if start and j == 12:
                    act.wait_ge(w_in, 16)
                    copy(W[:, :, HI, :], w1_raw).then_inc(w_hi, 1)
                if start and j == 14:
                    act.wait_ge(wa_in, 16)
                    copy(WA[:, :, HI, :], wa_raw).then_inc(wa_hi, 1)
                if start and j == 7:
                    act.wait_ge(m_done, 1)
                    copy(M[:, :, HI, :], mP).then_inc(m_hi, 1)

            def sums(layer, e, f):
                if f == 0:
                    act.wait_ge(agg0_done, whole(layer, e) + 1)
                else:
                    act.wait_ge(adj_used, 2 * STEPS * (whole(layer, e) + 1))
                if later(e):
                    act.wait_ge(proj_done[layer], (2 if layer == 1 else TPB) * e)
                elif layer == 2:
                    act.wait_ge(proj_done[1], 2 * NB)
                copy(agg[:, f, HI, :], aggP[f][:, :]).then_inc(agg_hi, 1)

            def epilogue1(e, j):
                if j == 3:
                    act.wait_ge(src_in[1], 16 * (e + 1))
                    if later(e):
                        act.wait_ge(proj_done[1], 2 * e)
                    copy(src[:, :, HI, :], src_raw[:, :, :]).then_inc(src_hi[1], 1)
                if j in (8, 9):
                    f = j - 8
                    act.wait_ge(proj_done[1], 2 * e + f + 1)
                    if later(e):
                        act.wait_ge(turn_done[1], 2 * e)
                        act.wait_ge(outT_out[1], 16 * e)
                    else:
                        act.wait_ge(x_lo, NX)
                    nc.scalar.activation(outT[:, f, :], projP[f][:, :], ACT.Relu).then_inc(outT_ready[1], 1)
                if j == 10:
                    act.wait_ge(outT_ready[1], 2 * e + 2)
                    store(h1T_dram, e, outT[:, :, :].rearrange("p f n -> p (f n)")).then_inc(outT_out[1], 16)
                if is_static(e) and e == NB - 1 and j == 11:
                    act.wait_ge(w_in, 32)
                    act.wait_ge(proj_done[1], 2 * NB)
                    copy(W[:, :, HI, :], w2_raw).then_inc(w_hi, 1)
                if j == 12:
                    for r in range(2):
                        act.wait_ge(turn_done[1], 2 * e + r + 1)
                        copy(H[:, ds(TPB * e + 2 * r, 2), HI, :],
                             turnP[r][:, :].rearrange("p (t n) -> p t n", t=2)).then_inc(made_hi[1], 1)

            def epilogue2(e, j):
                if j == 2 and later(e):
                    made_high(e - 1)
                if j == 3:
                    act.wait_ge(src_in[2], 16 * (e + 1))
                    if later(e):
                        act.wait_ge(att_done, 2 * e)
                    copy(src[:, :, HI, :], src_raw[:, :, :]).then_inc(src_hi[2], 1)
                if j in (7, 9, 11, 13):
                    k = (j - 7) // 2
                    n = TPB * e + k
                    act.wait_ge(x1_ready, n + 1)
                    store(x1_dram, n, x1[:, k % 2, :]).then_inc(x1_out[k % 2], 16)
                transposed(e, j)

            def made_high(w):
                for r in range(2):
                    act.wait_ge(att_done, 2 * w + r + 1)
                    copy(X[:, ds(TPB * w + 2 * r, 2), HI, :],
                         projP[r][:, :].rearrange("p (t n) -> p t n", t=2)).then_inc(made_hi[2], 1)

            def transposed(e, j):
                if j == 13:
                    act.wait_ge(turn_done[2], TPB * e + TPB)
                    act.wait_ge(proj_done[2], TPB * e + TPB)
                    for f in range(FT):
                        copy(src[:, f, HI, :], turnP[f][:, :]).then_inc(x1T_hi, 1)
                if j in (14, 15):
                    f = j - 14
                    act.wait_ge(x1T_lo, 2 * e + f + 1)
                    if later(e):
                        act.wait_ge(outT_out[2], 16 * e)
                    else:
                        act.wait_ge(outT_out[1], 16 * NB)
                    copy(outT[:, f, :], turnP[f][:, :]).then_inc(outT_ready[2], 1)
                if j == 15:
                    act.wait_ge(outT_ready[2], 2 * e + 2)
                    store(x1T_dram, e, outT[:, :, :].rearrange("p f n -> p (f n)")).then_inc(outT_out[2], 16)
            def finish(e):
                def early(c):
                    act.wait_ge(adj_used, 4 * STEPS * NB)
                    act.wait_ge(xt_in[c % RAW], 16 * (c // RAW + 1))
                    copy(XT[:, :, HI, c * CH:(c + 1) * CH], raw[:, c % RAW, :].rearrange("p (f n) -> p f n", f=FT))\
                        .then_inc(xt_hi, 1)

                def x1_store(k):
                    act.wait_ge(x1_ready, TPB * e + k + 1)
                    store(x1_dram, TPB * e + k, tail_x1[k]).then_inc(x1_out[k % 2], 16)

                sums(2, e, 0)
                sums(2, e, 1)
                early(0)
                early(1)
                act.wait_ge(src_in[2], 16 * (e + 1))
                act.wait_ge(att_done, 2 * e)
                for f in range(FT):
                    copy(src[:, f, HI, :], src_raw[:, f, :]).then_inc(src_hi[2], 1)
                made_high(e - 1)
                early(2)
                early(3)
                x1_store(0)
                early(4)
                for k in range(1, TPB):
                    x1_store(k)
                for j in range(13, STEPS):
                    transposed(e, j)
                early(5)
                early(6)
                made_high(e)

            walk(act, stream, epilogue1, epilogue2, finish)
            act.wait_ge(outT_out[2], 16 * NB)
            for s in range(2):
                act.wait_ge(x1_out[s], 16 * NT // 2)

        @block.vector
        def _(dve):
            def low(out, value, high):
                return nc.vector.tensor_tensor(out, value, high.bitcast(F32), ALU.subtract)

            def stream(layer, b, j):
                g = STEPS * whole(layer, b) + j
                start = layer == 1 and is_static(b) and b == 0
                if start and j % 2 == 0:
                    i = j // 2
                    at = slice(i * XS, (i + 1) * XS)
                    dve.wait_ge(x_hi, i + 1)
                    low(X[:, at, LO, :], x_raw[i % 2], X[:, at, HI, :]).then_inc(x_lo, 1)
                for t in range(2):
                    at = 2 * (j % 2) + t
                    dve.wait_ge(adj_hi, 2 * g + t + 1)
                    low(adj[:, at, LO, :], raw[:, j % RAW, t * ROWS:(t + 1) * ROWS], adj[:, at, HI, :])\
                        .then_inc(adj_lo, 1)
                    if j < FT and t == 0 and not start:
                        sums(*before(layer, b), j)
                if start and j == 12:
                    dve.wait_ge(w_hi, 1)
                    low(W[:, :, LO, :], w1_raw, W[:, :, HI, :]).then_inc(w_lo, 1)
                if start and j == 3:
                    dve.wait_ge(z_done, 1)
                    nc.vector.tensor_copy(z, zP).then_inc(z_ready, 1)
                if start and j == 14:
                    dve.wait_ge(wa_hi, 1)
                    low(WA[:, :, LO, :], wa_raw, WA[:, :, HI, :]).then_inc(wa_lo, 1)
                if start and j == 7:
                    dve.wait_ge(m_hi, 1)
                    low(M[:, :, LO, :], mP, M[:, :, HI, :]).then_inc(m_lo, 1)

            def sums(layer, e, f):
                dve.wait_ge(agg_hi, 2 * whole(layer, e) + f + 1)
                low(agg[:, f, LO, :], aggP[f][:, :], agg[:, f, HI, :]).then_inc(agg_lo, 1)

            def source(layer, e):
                dve.wait_ge(src_hi[layer], e + 1)
                low(src[:, :, LO, :], src_raw[:, :, :], src[:, :, HI, :]).then_inc(src_lo[layer], 1)

            def made_low(layer, made, banks, w):
                for r in range(2):
                    at = ds(TPB * w + 2 * r, 2)
                    dve.wait_ge(made_hi[layer], 2 * w + r + 1)
                    low(made[:, at, LO, :], banks[r][:, :].rearrange("p (t n) -> p t n", t=2), made[:, at, HI, :])\
                        .then_inc(made_lo[layer], 1)

            def epilogue1(e, j):
                if j == 3:
                    source(1, e)
                if is_static(e) and e == NB - 1 and j == 11:
                    dve.wait_ge(w_hi, 2)
                    low(W[:, :, LO, :], w2_raw, W[:, :, HI, :]).then_inc(w_lo, 1)
                if j == 12:
                    made_low(1, H, turnP, e)

            def epilogue2(e, j):
                if j == 2 and later(e):
                    made_low(2, X, projP, e - 1)
                if j == 3:
                    source(2, e)
                if j in (5, 7, 9, 11):
                    k = (j - 5) // 2
                    add_rows(e, k, projP[k % 2])
                if j in (6, 8, 10, 12):
                    normalise(e, (j - 6) // 2)
                if j in (13, 14):
                    transposed_low(e, j - 13)

            def add_rows(e, k, bank):
                n, s = TPB * e + k, k % 2
                dve.wait_ge(proj_done[2], n + 1)
                dve.wait_ge(rows_in[s], 16 * (TPB // 2 * e + k // 2 + 1))
                if not is_static(e) or n >= 2:
                    dve.wait_ge(x1_ready, n - 1)
                nc.vector.scalar_tensor_tensor(out=y[:, s, :], in0=bank[:, 0:D], scalar=0.0,
                                               in1=xn[:, s, :], op0=ALU.max, op1=ALU.add).then_inc(y_ready, 1)
                dve.wait_ge(y_ready, n + 1)
                nc.vector.bn_stats(stats[:, s, :], y[:, s, :]).then_inc(stats_ready, 1)
                dve.wait_ge(stats_ready, n + 1)
                nc.vector.memset(tick[:, :], 0.0)
                nc.vector.bn_aggr(mv[:, s, :], stats[:, s, :]).then_inc(mv_ready, 1)
                dve.wait_ge(mv_ready, n + 1)
                nc.vector.tensor_scalar_add(veps[:, s, :], mv[:, s, 1:2], EPS).then_inc(veps_ready, 1)

            def normalise(e, k, own=None):
                n, s = TPB * e + k, k % 2
                dve.wait_ge(rstd_ready, n + 1)
                if own is not None:
                    dve.wait_ge(src_lo[2], e + FT)
                elif not is_static(e) or n >= 2:
                    dve.wait_ge(x1_out[s], 16 * (TPB // 2 * e + k // 2))
                    dve.wait_ge(turn_done[2], n - 1)
                elif n == 0:
                    dve.wait_ge(wa_lo, 1)
                nc.vector.tensor_scalar(x1[:, s, :] if own is None else own, y[:, s, :], mv[:, s, 0:1], rstd[:, s, :],
                                        ALU.subtract, ALU.mult).then_inc(x1_ready, 1)

            def transposed_low(e, f):
                dve.wait_ge(x1T_hi, 2 * e + f + 1)
                low(src[:, f, LO, :], turnP[f][:, :], src[:, f, HI, :]).then_inc(x1T_lo, 1)

            def finish(e):
                def early(c):
                    at = slice(c * CH, (c + 1) * CH)
                    dve.wait_ge(xt_hi, c + 1)
                    low(XT[:, :, LO, at], raw[:, c % RAW, :].rearrange("p (f n) -> p f n", f=FT), XT[:, :, HI, at])\
                        .then_inc(xt_lo, 1)

                sums(2, e, 0)
                sums(2, e, 1)
                early(DVE_EARLY[0])
                for f in range(FT):
                    dve.wait_ge(src_hi[2], e + f + 1)
                    low(src[:, f, LO, :], src_raw[:, f, :], src[:, f, HI, :]).then_inc(src_lo[2], 1)
                made_low(2, X, projP, e - 1)
                add_rows(e, 0, tail_banks[0])
                for k in range(1, TPB):
                    add_rows(e, k, tail_banks[k])
                    normalise(e, k - 1, tail_x1[k - 1] if k > 2 else None)
                normalise(e, TPB - 1, tail_x1[TPB - 1])
                early(DVE_EARLY[1])
                for f in range(FT):
                    transposed_low(e, f)
                for c in DVE_EARLY[2:]:
                    early(c)
                made_low(2, X, projP, e)

            walk(dve, stream, epilogue1, epilogue2, finish)

        @block.tensor
        def _(pe):
            def three(out, stat, mov, start, stop):
                nc.tensor.matmul(out, stat(HI), mov(HI), start=start, stop=False)
                nc.tensor.matmul(out, stat(HI), mov(LO), start=False, stop=False)
                return nc.tensor.matmul(out, stat(LO), mov(HI), start=False, stop=stop)

            def small(out, stat, mov):
                for o in range(FT):
                    for k in range(FT):
                        last = nc.tensor.matmul(out[:, o, :], stat[:, k, o * P:(o + 1) * P], mov[:, k, :],
                                                start=k == 0, stop=k == FT - 1)
                return last

            T = 2 * STEPS
            ORDER = {0: [(0, 0), (1, 0)],
                     1: [(2, 0), (0, 1), (1, 1), (2, 1), (3, 0), (3, 1)],
                     STEPS - 2: [(T - 4, 0), (T - 4, 1), (T - 3, 0)],
                     STEPS - 1: [(T - 2, 0), (T - 1, 0), (T - 3, 1), (T - 2, 1), (T - 1, 1)]}

            def stream(layer, b, j):
                node = X if layer == 1 else H
                start = layer == 1 and is_static(b) and b == 0
                if start and j % 2 == 0:
                    pe.wait_ge(x_lo, j // 2 + 1)
                if layer == 2 and is_static(b) and b == 0:
                    if j == 0:
                        pe.wait_ge(made_lo[1], 2 * NB - 2)
                    if j == STEPS - 2:
                        pe.wait_ge(made_lo[1], 2 * NB)
                for i, f in ORDER.get(j, [(2 * j + t, f) for t in range(2) for f in range(FT)]):
                    if f == 0:
                        pe.wait_ge(adj_lo, 2 * STEPS * whole(layer, b) + i + 1)
                    if i == 0 and not start:
                        pe.wait_ge(agg_lo, 2 * whole(layer, b) + f - 1)
                    last = three(aggP[f][:, :],
                                 lambda h: node[:, i, h, f * P:(f + 1) * P],
                                 lambda h: adj[:, i % 4, h, :], i == 0, i == 2 * STEPS - 1)
                    if f == 1:
                        last.then_inc(adj_used, 1)
                    elif i == 2 * STEPS - 1:
                        last.then_inc(agg0_done, 1)
                if start and j == 2:
                    pe.wait_ge(t_in, 32)
                    small(zP, uT_raw, waT_raw).then_inc(z_done, 1)
                if start and j == 5:
                    pe.wait_ge(z_ready, 1)
                    small(mP, waT_raw, z).then_inc(m_done, 1)

            def epilogue1(e, j):
                if j in (5, 6):
                    o = j - 5
                    pe.wait_ge(agg_lo, 2 * e + 2)
                    pe.wait_ge(src_lo[1], e + 1)
                    if later(e):
                        pe.wait_ge(outT_ready[1], 2 * e - 1 + o)
                    else:
                        pe.wait_ge(w_lo, 1)
                        pe.wait_ge(m_lo, 1)
                    for kt in range(2 * FT):
                        part = src if kt < FT else agg
                        last = three(projP[o][:, :], lambda h: W[:, kt, h, o * P:(o + 1) * P],
                                     lambda h: part[:, kt % FT, h, :], kt == 0, kt == 2 * FT - 1)
                    last.then_inc(proj_done[1], 1)
                if j == 10:
                    if not later(e):
                        pe.wait_ge(constants, 2)
                    for r in range(2):
                        pe.wait_ge(outT_ready[1], 2 * e + 2)
                        if later(e):
                            pe.wait_ge(made_lo[1], 2 * e - 1 + r)
                        for q in range(2):
                            for f in range(FT):
                                i = 2 * r + q
                                last = nc.tensor.transpose(turnP[r][:, q * D + f * P:q * D + (f + 1) * P],
                                                           outT[:, f, i * P:(i + 1) * P], ident[:, :])
                        last.then_inc(turn_done[1], 1)

            def epilogue2(e, j):
                if j in (3, 5, 7, 9):
                    k = (j - 3) // 2
                    n = TPB * e + k
                    if k == 0:
                        pe.wait_ge(agg_lo, 2 * whole(2, e) + 2)
                        pe.wait_ge(src_lo[2], e + 1)
                        if not later(e):
                            pe.wait_ge(w_lo, 2)
                    if k >= 2:
                        pe.wait_ge(y_ready, n - 1)
                    elif later(e):
                        pe.wait_ge(made_lo[2], 2 * e - 1 + k)
                    project(projP[k % 2], k, range(2 * FT), True, True).then_inc(proj_done[2], 1)
                if j in (6, 8, 10, 12):
                    turn(e, (j - 6) // 2, x1[:, (j - 6) // 2 % 2, :])
                if j == 15:
                    times_wa(e)

            def project(bank, k, kts, start, stop):
                for kt in kts:
                    part = src if kt < FT else agg
                    last = three(bank[:, 0:D], lambda h: part[:, kt % FT, h, k * P:(k + 1) * P],
                                 lambda h: W[:, kt, h, :], start and kt == kts[0], stop and kt == kts[-1])
                return last

            def turn(e, k, rows):
                n = TPB * e + k
                pe.wait_ge(x1_ready, n + 1)
                if k == 0 and later(e):
                    pe.wait_ge(outT_ready[2], 2 * e)
                for f in range(FT):
                    last = nc.tensor.transpose(turnP[f][:, k * P:(k + 1) * P],
                                               rows[:, f * P:(f + 1) * P], ident[:, :])
                last.then_inc(turn_done[2], 1)

            def times_wa(e):
                pe.wait_ge(x1T_lo, 2 * e + 2)
                pe.wait_ge(y_ready, TPB * e + TPB)
                if not later(e):
                    pe.wait_ge(wa_lo, 1)
                for r in range(2):
                    for q in range(2):
                        i = 2 * r + q
                        for f in range(FT):
                            last = three(projP[r][:, q * D:(q + 1) * D],
                                         lambda h: src[:, f, h, i * P:(i + 1) * P],
                                         lambda h: WA[:, f, h, :], f == 0, f == FT - 1)
                    last.then_inc(att_done, 1)

            def finish(e):
                def terms(k, kts):
                    return project(tail_banks[k], k, kts, kts[0] == FT, kts[0] == 0)

                of_agg, of_src = range(FT, 2 * FT), range(FT)
                pe.wait_ge(agg_lo, 2 * whole(2, e) + 2)
                terms(0, of_agg)
                terms(1, of_agg)
                pe.wait_ge(src_lo[2], e + FT)
                terms(0, of_src).then_inc(proj_done[2], 1)
                terms(1, of_src).then_inc(proj_done[2], 1)
                for k in (2, 3):
                    pe.wait_ge(made_lo[2], 2 * e - 3 + k)
                    terms(k, of_agg)
                    terms(k, of_src).then_inc(proj_done[2], 1)
                for k in range(TPB):
                    turn(e, k, tail_x1[k])
                times_wa(e)

            walk(pe, stream, epilogue1, epilogue2, finish)


def attention(nc, keep, adj_dram, x1T_dram, x1_dram, out):
    H, XT, M, ident = keep["X"], x1T_view(keep), keep["M"], keep["ident"]
    SLOTS = 16
    BODY = 16
    LAST = NT * NC

    with ExitStack() as ctx:
        def sb(name, shape, dt):
            return ctx.enter_context(nc.sbuf_tensor(name, shape, dt))

        def ps(name, shape=(P, 512)):
            return ctx.enter_context(nc.psum_tensor(name, list(shape), F32))

        def sem(name):
            return ctx.enter_context(nc.semaphore(name))

        adj = sb("adj", [P, SLOTS, CH], F32)
        pm = sb("pm", [P, NC + 1, CH], F32)
        bias = sb("bias", [P, 2, CH], BF16)
        turned = sb("turned", [P, 2, 2, CH], F32R)
        strip = sb("strip", [P, (2 * NC - 1) * P], BF16)
        q = sb("q", [P, FT, 2, 2 * P], F32R)
        mx, sums = sb("mx", [P, 2, NC], F32), sb("sums", [P, 2, NC], F32)
        mrow, nmax = sb("mrow", [P, 2, 1], F32), sb("nmax", [P, 2, 1], F32)
        rsum, rinv = sb("rsum", [P, 2, 1], F32), sb("rinv", [P, 2, 1], F32)
        tick = sb("tick_att", [P, 1], F32)
        cross = sb("cross", [P, D], F32)
        both = sb("both", [P, D], F32)
        x1 = sb("x1_rows", [P, 2, D], F32)
        y = sb("y_att", [P, D], F32)
        fin = sb("fin", [P, 2, D], F32)
        stats, mv = sb("stats_att", [P, 2, 6], F32), sb("mv_att", [P, 2, 2], F32)
        veps, rstd = sb("veps_att", [P, 2, 1], F32), sb("rstd_att", [P, 2, 1], F32)
        scoreP = [ps(f"scoreP{i}") for i in range(4)]
        turnP = [ps("turn_att0"), ps("turn_att1")]
        accP = ps("accP")
        qP = ps("qP", (P, FT, 2 * P))

        adj_in = [sem(f"adj_in{i}") for i in range(SLOTS // 2)]
        xt_in = [sem(f"xt_in{i}") for i in range(NC - EARLY)]
        x1_in = [sem("x1_in0"), sem("x1_in1")]
        out_sent = [sem("out_sent0"), sem("out_sent1")]
        xt_hi, xt_lo = sem("xt_hi"), sem("xt_lo")
        zeroed, strip_ready = sem("zeroed_strip"), sem("strip_ready")
        q_done, q_hi, q_lo = sem("q_done"), sem("q_hi"), sem("q_lo")
        diag_added, bias_ready = sem("diag_added"), sem("bias_ready")
        scores_done, masked, mrow_ready, nmax_ready = (sem(n) for n in
                                                       ("scores_done", "masked", "mrow_ready", "nmax_ready"))
        exp_done, weighted, turn_done = sem("exp_done"), sem("weighted"), sem("turn_att_done")
        turned_hi, turned_lo, av_done = sem("turned_hi"), sem("turned_lo"), sem("av_done")
        cross_ready, acc_read, rsum_ready, rinv_ready = (sem(n) for n in
                                                         ("cross_ready", "acc_read", "rsum_ready", "rinv_ready"))
        y_ready, stats_ready, mv_ready = sem("y_att_ready"), sem("stats_att_ready"), sem("mv_att_ready")
        veps_ready, rstd_ready, fin_ready = sem("veps_att_ready"), sem("rstd_att_ready"), sem("fin_ready")

        def slot(a):
            return NC if a == 2 * NC - 1 else a % NC

        def walk(eng, step, tail=BODY + 2):
            for s in range(BODY):
                step(0, s)
            with eng.Fori(1, NT // 2 - 1) as k:
                for s in range(BODY):
                    step(k, s)
            for s in range(BODY + tail):
                step(NT // 2 - 1 + s // BODY, s % BODY)

        def live(k, s, back):
            return not is_static(k) or 0 <= BODY * k + s - back < LAST

        block = ctx.enter_context(nc.Block())

        @block.sync
        def _(sp):
            def adj_load(k, s8):
                w = SLOTS // 2 * k + s8
                sp.dma_start(adj[:, 2 * s8:2 * s8 + 2, :].rearrange("p c n -> p (c n)"),
                             adj_dram[ds(w, 1), :, :].rearrange("o p n -> (o p) n")).then_inc(adj_in[s8], 16)

            def x1_load(n, s):
                sp.dma_start(x1[:, s, :], x1_dram[ds(n, 1), :, :].rearrange("o p n -> (o p) n"))\
                    .then_inc(x1_in[s], 16)

            for s8 in range(4):
                adj_load(0, s8)
                if s8 < NC - EARLY:
                    sp.dma_start(adj[:, 8 + 2 * s8:10 + 2 * s8, :], x1T_dram[EARLY + s8, :, :]
                                 .rearrange("p (f n) -> p f n", f=FT)).then_inc(xt_in[s8], 16)
            for n in range(2):
                x1_load(n, n)
            for s8 in range(4, 8):
                if s8 - 4 < NC - EARLY:
                    sp.wait_ge(xt_lo, s8 - 3)
                adj_load(0, s8)

            def store(n, s):
                sp.wait_ge(fin_ready, n + 1)
                sp.dma_start(out[ds(n, 1), :, :].rearrange("o p n -> (o p) n"), fin[:, s, :])\
                    .then_inc(out_sent[s], 16)

            def turnover(n, u):
                store(n, u)
                sp.wait_ge(y_ready, n + 1)
                x1_load(n + 2, u)

            def pair(k):
                for s8 in range(8):
                    sp.wait_ge(weighted, 16 * k + 2 * s8 - 14)
                    adj_load(k, s8)
                    if s8 == 3 and (not is_static(k) or k >= 2):
                        turnover(2 * k - 3, 1)
                    if s8 == 7:
                        turnover(2 * k - 2, 0)

            pair(1)
            with sp.Fori(2, NT // 2) as k:
                pair(k)
            turnover(NT - 3, 1)
            store(NT - 2, 0)
            store(NT - 1, 1)
            for s in range(2):
                sp.wait_ge(out_sent[s], 16 * NT // 2)

        @block.gpsimd
        def _(pool):
            def diag(k, s, ahead):
                p, s = k + (s + ahead) // BODY, (s + ahead) % BODY
                u, c = s // NC, s % NC
                pool.wait_ge(adj_in[s // 2], 16 * (p + 1))
                col = s * CH + (p % 2) * (2 * P) + u * P
                off = (NC - 1 - c) * P + (p // 2) * P
                at = adj[:, :, :].rearrange("p c n -> p (c n)")[:, ds(col, P)]
                nc.gpsimd.tensor_tensor(at, at, strip[:, ds(off, P)], ALU.add).then_inc(diag_added, 1)

            def step(k, s):
                if live(k, s, 8):
                    t = BODY * k + s - 8
                    a = (s - 8) % BODY
                    pool.wait_ge(exp_done, t + 1)
                    nc.gpsimd.tensor_tensor(pm[:, slot(a), :], pm[:, slot(a), :], adj[:, a, :], ALU.mult)\
                        .then_inc(weighted, 1)
                if live(k, s, -4):
                    diag(k, s, 4)
                if s % NC == 4 and (not is_static(k) or 0 <= 2 * k + s // NC - 2 < NT):
                    n = 2 * k + s // NC - 2
                    r = s // NC
                    pool.wait_ge(veps_ready, n + 1)
                    nc.gpsimd.tensor_tensor(rstd[:, r, :], veps[:, r, :], keep["neg_half"][:, :], ALU.pow)\
                        .then_inc(rstd_ready, 1)

            nc.gpsimd.memset(strip[:, :], 0.0).then_inc(zeroed, 1)
            pool.wait_ge(zeroed, 1)
            mid = strip[:, (NC - 1) * P:NC * P]
            nc.gpsimd.affine_select(out=mid, in_=mid, compare_op=ALU.not_equal, fill=1.0, base=0,
                                    pattern=[[-1, P]], channel_multiplier=1).then_inc(strip_ready, 1)
            pool.wait_ge(strip_ready, 1)
            for s in range(4):
                diag(0, s, 0)
            walk(pool, step)

        @block.scalar
        def _(act):
            def xt_high(i):
                act.wait_ge(xt_in[i], 16)
                nc.scalar.activation(XT[:, :, HI, (EARLY + i) * CH:(EARLY + i + 1) * CH],
                                     adj[:, 8 + 2 * i:10 + 2 * i, :], ACT.Copy).then_inc(xt_hi, 1)

            def q_high(pair, u):
                act.wait_ge(q_done, pair + 1)
                at = slice(u * P, (u + 1) * P)
                nc.scalar.activation(q[:, :, HI, at], qP[:, :, at], ACT.Copy).then_inc(q_hi, 1)

            def step(k, s):
                if is_static(k) and k == 0 and s < NC - EARLY:
                    xt_high(s)
                if s == 12 and (not is_static(k) or k + 1 < NT // 2):
                    act.wait_ge(scores_done, BODY * k + NC)
                    q_high(k + 1, 0)
                if s == 1 and (not is_static(k) or 1 <= k < NT // 2):
                    act.wait_ge(scores_done, BODY * k)
                    q_high(k, 1)
                if live(k, s, 8):
                    t, a = BODY * k + s - 8, (s - 8) % BODY
                    u, c = a // NC, a % NC
                    if c == 0:
                        m = 2 * k + (s - 8) // NC
                        act.wait_ge(nmax_ready, m + 1)
                    nc.scalar.activation(pm[:, slot(a), :], pm[:, slot(a), :], ACT.Exp, bias=nmax[:, u, :],
                                         accum_out=sums[:, u, c:c + 1]).then_inc(exp_done, 1)
                if live(k, s, 9):
                    t, c = BODY * k + s - 9, (s - 9) % NC
                    act.wait_ge(turn_done, t + 1)
                    if not is_static(k) or t >= 2:
                        act.wait_ge(av_done, t - 1)
                    nc.scalar.activation(turned[:, c % 2, HI, :], turnP[c % 2][:, :], ACT.Copy)\
                        .then_inc(turned_hi, 1)
                if s % NC == 1 and (not is_static(k) or 0 <= 2 * k + s // NC - 2 < NT):
                    n = 2 * k + s // NC - 2
                    act.wait_ge(av_done, NC * n + NC)
                    if not is_static(k) or n >= 1:
                        act.wait_ge(acc_read, n)
                    nc.scalar.activation(cross[:, :], accP[:, D:2 * D], ACT.Copy).then_inc(cross_ready, 1)

            q_high(0, 0)
            q_high(0, 1)
            walk(act, step)

        @block.vector
        def _(dve):
            def low(out, value, high):
                return nc.vector.tensor_tensor(out, value, high, ALU.subtract)

            def xt_low(i):
                at = slice((EARLY + i) * CH, (EARLY + i + 1) * CH)
                dve.wait_ge(xt_hi, i + 1)
                low(XT[:, :, LO, at], adj[:, 8 + 2 * i:10 + 2 * i, :], XT[:, :, HI, at].bitcast(F32)).then_inc(xt_lo, 1)

            def q_low(pair, u):
                dve.wait_ge(q_hi, 2 if is_static(pair) and pair == 0 else 2 * pair + u + 1)
                at = slice(u * P, (u + 1) * P)
                low(q[:, :, LO, at], qP[:, :, at], q[:, :, HI, at].bitcast(F32)).then_inc(q_lo, 1)

            def mask_bias(k, s, ahead):
                t, a = BODY * k + s + ahead, (s + ahead) % BODY
                if not is_static(k) or t >= 2:
                    dve.wait_ge(masked, t - 1)
                dve.wait_ge(diag_added, t + 1)
                nc.vector.tensor_scalar(bias[:, a % 2, :], adj[:, a, :], 0.0, -BIG, ALU.is_le, ALU.mult)\
                    .then_inc(bias_ready, 1)

            def step(k, s):
                if is_static(k) and k == 0 and s < NC - EARLY:
                    xt_low(s)
                if live(k, s, 9):
                    t, c = BODY * k + s - 9, (s - 9) % NC
                    dve.wait_ge(turned_hi, t + 1)
                    low(turned[:, c % 2, LO, :], turnP[c % 2][:, :], turned[:, c % 2, HI, :].bitcast(F32))\
                        .then_inc(turned_lo, 1)
                if s % NC == 1 and (not is_static(k) or 0 <= 2 * k + s // NC - 2 < NT):
                    n = 2 * k + s // NC - 2
                    dve.wait_ge(cross_ready, n + 1)
                    if not is_static(k) or n >= 1:
                        dve.wait_ge(y_ready, n)
                    nc.vector.tensor_tensor(both[:, :], accP[:, 0:D], cross[:, :], ALU.add).then_inc(acc_read, 1)
                if live(k, s, 0):
                    t, u, c = BODY * k + s, s // NC, s % NC
                    dve.wait_ge(scores_done, t + 1)
                    dve.wait_ge(bias_ready, t + 1)
                    back = 2 * NC if c == NC - 1 else NC
                    if not is_static(k) or t >= back:
                        dve.wait_ge(turn_done, t - back + 1)
                    if not is_static(k) or t >= 1:
                        dve.wait_ge(masked, t)
                    nc.vector.memset(tick[:, :], 0.0)
                    nc.vector.tensor_tensor_reduce(out=pm[:, slot(s), :], in0=scoreP[s % 4][:, :],
                                                   in1=bias[:, s % 2, :], scale=1.0, scalar=-2.0 * BIG, op0=ALU.add, op1=ALU.max,
                                                   accum_out=mx[:, u, c:c + 1]).then_inc(masked, 1)
                    if c == NC - 1:
                        m = 2 * k + u
                        dve.wait_ge(masked, t + 1)
                        nc.vector.reduce_max(mrow[:, u, :], mx[:, u, :], AX.X).then_inc(mrow_ready, 1)
                        dve.wait_ge(mrow_ready, m + 1)
                        nc.vector.tensor_scalar_mul(nmax[:, u, :], mrow[:, u, :], -1.0).then_inc(nmax_ready, 1)
                if live(k, s, -1):
                    mask_bias(k, s, 1)
                if s == 12 and (not is_static(k) or k + 1 < NT // 2):
                    q_low(k + 1, 0)
                if s == 1 and (not is_static(k) or 1 <= k < NT // 2):
                    q_low(k, 1)
                if s % NC == 2 and (not is_static(k) or 0 <= 2 * k + s // NC - 2 < NT):
                    n, r = 2 * k + s // NC - 2, s // NC
                    nc.vector.reduce_sum(rsum[:, r, :], sums[:, r, :], AX.X).then_inc(rsum_ready, 1)
                    dve.wait_ge(rsum_ready, n + 1)
                    nc.vector.reciprocal(rinv[:, r, :], rsum[:, r, :]).then_inc(rinv_ready, 1)
                    dve.wait_ge(rinv_ready, n + 1)
                    dve.wait_ge(acc_read, n + 1)
                    dve.wait_ge(x1_in[r], 16 * k)
                    nc.vector.scalar_tensor_tensor(out=y[:, :], in0=both[:, :], scalar=rinv[:, r, :],
                                                   in1=x1[:, r, :], op0=ALU.mult, op1=ALU.add).then_inc(y_ready, 1)
                if s % NC == 3 and (not is_static(k) or 0 <= 2 * k + s // NC - 2 < NT):
                    n, r = 2 * k + s // NC - 2, s // NC
                    dve.wait_ge(y_ready, n + 1)
                    nc.vector.bn_stats(stats[:, r, :], y[:, :]).then_inc(stats_ready, 1)
                    dve.wait_ge(stats_ready, n + 1)
                    nc.vector.memset(tick[:, :], 0.0)
                    nc.vector.bn_aggr(mv[:, r, :], stats[:, r, :]).then_inc(mv_ready, 1)
                    dve.wait_ge(mv_ready, n + 1)
                    nc.vector.tensor_scalar_add(veps[:, r, :], mv[:, r, 1:2], EPS).then_inc(veps_ready, 1)
                if s % NC == 6 and (not is_static(k) or 0 <= 2 * k + s // NC - 2 < NT):
                    n, r = 2 * k + s // NC - 2, s // NC
                    dve.wait_ge(rstd_ready, n + 1)
                    if not is_static(k) or n >= 2:
                        dve.wait_ge(out_sent[r], 16 * (k - 1))
                    nc.vector.tensor_scalar(fin[:, r, :], y[:, :], mv[:, r, 0:1], rstd[:, r, :],
                                            ALU.subtract, ALU.mult).then_inc(fin_ready, 1)

            q_low(0, 0)
            q_low(0, 1)
            mask_bias(0, 0, 0)
            walk(dve, step)

        @block.tensor
        def _(pe):
            def three(out, stat, mov, start, stop):
                nc.tensor.matmul(out, stat(HI), mov(HI), start=start, stop=False)
                nc.tensor.matmul(out, stat(HI), mov(LO), start=False, stop=False)
                return nc.tensor.matmul(out, stat(LO), mov(HI), start=False, stop=stop)

            def q_pair(pair):
                for o in range(FT):
                    for f in range(FT):
                        last = three(qP[:, o, :], lambda h: M[:, f, h, o * P:(o + 1) * P],
                                     lambda h: XT[:, f, h, ds(2 * P * pair, 2 * P)], f == 0, f == FT - 1)
                last.then_inc(q_done, 1)

            def step(k, s):
                if live(k, s, 0):
                    t, u, c = BODY * k + s, s // NC, s % NC
                    if s == 0 or s == NC:
                        pe.wait_ge(q_lo, 2 * k + u + 1)
                    if is_static(k) and k == 0 and EARLY <= s < NC:
                        pe.wait_ge(xt_lo, s - EARLY + 1)
                    if not is_static(k) or t >= 4:
                        pe.wait_ge(masked, t - 3)
                    for f in range(FT):
                        last = three(scoreP[s % 4][:, :], lambda h: q[:, f, h, u * P:(u + 1) * P],
                                     lambda h: XT[:, f, h, c * CH:(c + 1) * CH], f == 0, f == FT - 1)
                    last.then_inc(scores_done, 1)
                if s == 8 and (not is_static(k) or k + 1 < NT // 2):
                    pe.wait_ge(q_lo, 2 * k + 2)
                    q_pair(k + 1)
                if live(k, s, 9):
                    t, a = BODY * k + s - 9, (s - 9) % BODY
                    c = a % NC
                    pe.wait_ge(weighted, t + 1)
                    if not is_static(k) or t >= 2:
                        pe.wait_ge(turned_lo, t - 1)
                    for i in range(CH // P):
                        last = nc.tensor.transpose(turnP[c % 2][:, i * P:(i + 1) * P],
                                                   pm[:, slot(a), i * P:(i + 1) * P], ident[:, :])
                    last.then_inc(turn_done, 1)
                if live(k, s, 10):
                    t, c = BODY * k + s - 10, (s - 10) % NC
                    pe.wait_ge(turned_lo, t + 1)
                    if c == 0:
                        m = 2 * k + (s - 10) // NC
                        if not is_static(k) or m >= 1:
                            pe.wait_ge(acc_read, m)
                    for i in range(CH // P):
                        j = c * (CH // P) + i
                        at = slice(i * P, (i + 1) * P)
                        nc.tensor.matmul(accP[:, :], turned[:, c % 2, HI, at],
                                         H[:, j, :, :].rearrange("p h n -> p (h n)"),
                                         start=j == 0, stop=False)
                        last = nc.tensor.matmul(accP[:, 0:D], turned[:, c % 2, LO, at], H[:, j, HI, :],
                                                start=False, stop=j == NT - 1)
                    last.then_inc(av_done, 1)

            q_pair(0)
            walk(pe, step)


def build(nc, x_nodes, x_rows, xT, adjT, adjN, w1, w2, wa, waT, uT, out):
    h1T = nc.dram_tensor("h1T", (NB, P, FT * ROWS), F32, kind="Internal").ap()
    x1T = nc.dram_tensor("x1T", (NB, P, FT * ROWS), F32, kind="Internal").ap()
    x1 = nc.dram_tensor("x1d", (NT, P, D), F32, kind="Internal").ap()
    with ExitStack() as ctx:
        def sb(where, name, shape, dt):
            return where.enter_context(nc.sbuf_tensor(name, shape, dt))

        keep = {
            "X": sb(ctx, "node_x", [P, NT, 2, D], F32R),
            "H": sb(ctx, "node_h", [P, NT, 2, D], F32R),
            "M": sb(ctx, "score_m", [P, FT, 2, D], F32R),
            "ident": sb(ctx, "ident", [P, P], F32),
            "neg_half": sb(ctx, "neg_half", [P, 1], F32),
        }
        with ExitStack() as first:
            keep["WA"] = sb(first, "wa_parts", [P, FT, 2, D], F32R)
            convolutions(nc, keep, adjT, xT, x_nodes, x_rows, w1, w2, wa, waT, uT, h1T, x1T, x1)
        attention(nc, keep, adjN, x1T, x1, out)


def kernel(x, adj, L0_gnn_W1, L0_gnn_W2, L1_gnn_W, L1_gnn_U):
    import numpy as np
    import concourse.bacc as bacc
    from concourse.bass_utils import run_bass_kernel_spmd

    x, adj = np.asarray(x), np.asarray(adj)
    tiles = lambda w: np.ascontiguousarray(np.asarray(w).reshape(-1, P, D).transpose(1, 0, 2))
    arrays = {
        "x_nodes": tiles(x),
        "x_rows": x.reshape(NT, P, D),
        "xT": np.ascontiguousarray(x.reshape(NB, ROWS, FT, P).transpose(0, 3, 2, 1)).reshape(NB, P, FT * ROWS),
        "adjT": np.ascontiguousarray(adj.reshape(NB, ROWS, STEPS, 2, P).transpose(0, 2, 4, 3, 1))
        .reshape(NB * STEPS, P, 2 * ROWS),
        "adjN": np.ascontiguousarray(adj.reshape(NT, P, NC // 2, 2 * CH).transpose(0, 2, 1, 3))
        .reshape(NT * NC // 2, P, 2 * CH),
        "w1": tiles(L0_gnn_W1),
        "w2": tiles(L0_gnn_W2),
        "wa": tiles(L1_gnn_W),
        "waT": tiles(np.asarray(L1_gnn_W).T),
        "uT": tiles(np.asarray(L1_gnn_U).T),
    }
    nc = bacc.Bacc("TRN2", target_bir_lowering=False, num_devices=1)
    args = [nc.dram_tensor(n, a.shape, mybir.dt.from_np(a.dtype), kind="ExternalInput").ap()
            for n, a in arrays.items()]
    out = nc.dram_tensor("out", (NT, P, D), F32, kind="ExternalOutput").ap()
    build(nc, *args, out)
    r = run_bass_kernel_spmd(nc, [arrays], core_ids=[0])
    return r.results[0]["out"].reshape(N, D)
```
